# Optimizing a Trainium2 kernel written in Bass

```python
import numpy as np
import jax
import jax.numpy as jnp

def _softmax(x, axis=-1):
    return jax.nn.softmax(x, axis=axis)

def _gelu(x):
    return jax.nn.gelu(x, approximate=True)

def _silu(x):
    return jax.nn.silu(x)

def _sigmoid(x):
    return jax.nn.sigmoid(x)

def _layernorm(x, axis=-1, eps=1e-05):
    m = jnp.mean(x, axis=axis, keepdims=True)
    v = jnp.var(x, axis=axis, keepdims=True)
    return (x - m) / jnp.sqrt(v + eps)

def _scatter_add(tgt, idx, src, axis=0):
    return tgt.at[idx].add(src)

def _segment_sum(src, seg, n):
    return jax.ops.segment_sum(src, seg, n)
kernel_name = 'mk_dlrm_tower_d1_rec_r8_f8828e'

def setup_inputs(seed: int=0):
    np.random.seed(seed)
    _w = jnp.asarray

    def _rec_inputs():
        import jax
        import jax.numpy as jnp
        _tk = jax.random.key(seed)
        dense_ctx = jax.random.normal(jax.random.fold_in(_tk, 190), (1024, 16), jnp.float32)
        ids = jnp.stack([jax.random.randint(jax.random.fold_in(_tk, 200 + f), (1024,), 0, v, jnp.int32) for f, v in enumerate([125000, 12500, 1000, 1000, 1000, 125000, 12500, 125000, 1250, 1000, 12500, 1250, 1250, 1000, 125000, 125000, 1250, 1000, 125000, 1000, 12500, 1000, 1250, 12500, 1250, 12500, 1000, 1250, 125000, 1000, 1250, 12500])], axis=1)
        tbl_0 = 0.05 * jax.random.normal(jax.random.fold_in(_tk, 500 + 0), (125000, 32), jnp.float32)
        tbl_1 = 0.05 * jax.random.normal(jax.random.fold_in(_tk, 500 + 1), (12500, 32), jnp.float32)
        tbl_2 = 0.05 * jax.random.normal(jax.random.fold_in(_tk, 500 + 2), (1000, 32), jnp.float32)
        tbl_3 = 0.05 * jax.random.normal(jax.random.fold_in(_tk, 500 + 3), (1000, 32), jnp.float32)
        tbl_4 = 0.05 * jax.random.normal(jax.random.fold_in(_tk, 500 + 4), (1000, 32), jnp.float32)
        tbl_5 = 0.05 * jax.random.normal(jax.random.fold_in(_tk, 500 + 5), (125000, 32), jnp.float32)
        tbl_6 = 0.05 * jax.random.normal(jax.random.fold_in(_tk, 500 + 6), (12500, 32), jnp.float32)
        tbl_7 = 0.05 * jax.random.normal(jax.random.fold_in(_tk, 500 + 7), (125000, 32), jnp.float32)
        tbl_8 = 0.05 * jax.random.normal(jax.random.fold_in(_tk, 500 + 8), (1250, 32), jnp.float32)
        tbl_9 = 0.05 * jax.random.normal(jax.random.fold_in(_tk, 500 + 9), (1000, 32), jnp.float32)
        tbl_10 = 0.05 * jax.random.normal(jax.random.fold_in(_tk, 500 + 10), (12500, 32), jnp.float32)
        tbl_11 = 0.05 * jax.random.normal(jax.random.fold_in(_tk, 500 + 11), (1250, 32), jnp.float32)
        tbl_12 = 0.05 * jax.random.normal(jax.random.fold_in(_tk, 500 + 12), (1250, 32), jnp.float32)
        tbl_13 = 0.05 * jax.random.normal(jax.random.fold_in(_tk, 500 + 13), (1000, 32), jnp.float32)
        tbl_14 = 0.05 * jax.random.normal(jax.random.fold_in(_tk, 500 + 14), (125000, 32), jnp.float32)
        tbl_15 = 0.05 * jax.random.normal(jax.random.fold_in(_tk, 500 + 15), (125000, 32), jnp.float32)
        tbl_16 = 0.05 * jax.random.normal(jax.random.fold_in(_tk, 500 + 16), (1250, 32), jnp.float32)
        tbl_17 = 0.05 * jax.random.normal(jax.random.fold_in(_tk, 500 + 17), (1000, 32), jnp.float32)
        tbl_18 = 0.05 * jax.random.normal(jax.random.fold_in(_tk, 500 + 18), (125000, 32), jnp.float32)
        tbl_19 = 0.05 * jax.random.normal(jax.random.fold_in(_tk, 500 + 19), (1000, 32), jnp.float32)
        tbl_20 = 0.05 * jax.random.normal(jax.random.fold_in(_tk, 500 + 20), (12500, 32), jnp.float32)
        tbl_21 = 0.05 * jax.random.normal(jax.random.fold_in(_tk, 500 + 21), (1000, 32), jnp.float32)
        tbl_22 = 0.05 * jax.random.normal(jax.random.fold_in(_tk, 500 + 22), (1250, 32), jnp.float32)
        tbl_23 = 0.05 * jax.random.normal(jax.random.fold_in(_tk, 500 + 23), (12500, 32), jnp.float32)
        tbl_24 = 0.05 * jax.random.normal(jax.random.fold_in(_tk, 500 + 24), (1250, 32), jnp.float32)
        tbl_25 = 0.05 * jax.random.normal(jax.random.fold_in(_tk, 500 + 25), (12500, 32), jnp.float32)
        tbl_26 = 0.05 * jax.random.normal(jax.random.fold_in(_tk, 500 + 26), (1000, 32), jnp.float32)
        tbl_27 = 0.05 * jax.random.normal(jax.random.fold_in(_tk, 500 + 27), (1250, 32), jnp.float32)
        tbl_28 = 0.05 * jax.random.normal(jax.random.fold_in(_tk, 500 + 28), (125000, 32), jnp.float32)
        tbl_29 = 0.05 * jax.random.normal(jax.random.fold_in(_tk, 500 + 29), (1000, 32), jnp.float32)
        tbl_30 = 0.05 * jax.random.normal(jax.random.fold_in(_tk, 500 + 30), (1250, 32), jnp.float32)
        tbl_31 = 0.05 * jax.random.normal(jax.random.fold_in(_tk, 500 + 31), (12500, 32), jnp.float32)
        _rk = jax.random.fold_in(_tk, 7)
        W_top1 = 0.0606339 * jax.random.normal(jax.random.fold_in(_tk, 801), (272, 512), jnp.float32)
        W_top2 = 0.0441942 * jax.random.normal(jax.random.fold_in(_tk, 802), (512, 256), jnp.float32)
        W_top3 = 0.0625 * jax.random.normal(jax.random.fold_in(_tk, 803), (256, 1), jnp.float32)
        b_top1 = jnp.zeros((512,), jnp.float32)
        b_top2 = jnp.zeros((256,), jnp.float32)
        return (dense_ctx, ids, tbl_0, tbl_1, tbl_2, tbl_3, tbl_4, tbl_5, tbl_6, tbl_7, tbl_8, tbl_9, tbl_10, tbl_11, tbl_12, tbl_13, tbl_14, tbl_15, tbl_16, tbl_17, tbl_18, tbl_19, tbl_20, tbl_21, tbl_22, tbl_23, tbl_24, tbl_25, tbl_26, tbl_27, tbl_28, tbl_29, tbl_30, tbl_31, W_top1, b_top1, W_top2, b_top2, W_top3)
    dense_ctx, ids, tbl_0, tbl_1, tbl_2, tbl_3, tbl_4, tbl_5, tbl_6, tbl_7, tbl_8, tbl_9, tbl_10, tbl_11, tbl_12, tbl_13, tbl_14, tbl_15, tbl_16, tbl_17, tbl_18, tbl_19, tbl_20, tbl_21, tbl_22, tbl_23, tbl_24, tbl_25, tbl_26, tbl_27, tbl_28, tbl_29, tbl_30, tbl_31, W_top1, b_top1, W_top2, b_top2, W_top3 = _rec_inputs()

    def _L0_rec_setup():
        import jax, jax.numpy as jnp
        import numpy as np
        B, F, D = (512, 32, 32)
        LAYER_SIZE = [128, 128]

        def _cin_forward(inputs, filters):
            x0 = inputs
            prev = inputs
            outs = []
            for W in filters:
                z = jnp.einsum('bhd,bmd->bhmd', x0, prev)
                b, h, m, d = z.shape
                z = z.reshape(b, h * m, d)
                cur = jnp.einsum('bpd,pn->bnd', z, W[0])
                cur = jax.nn.relu(cur)
                prev = cur
                outs.append(cur)
            result = jnp.concatenate(outs, axis=1)
            return jnp.sum(result, axis=-1)
        key = jax.random.key(seed)
        k1, k2, k3 = jax.random.split(key, 3)
        inputs = jax.random.normal(k1, (B, F, D), dtype=jnp.float32)
        field_nums = [F] + LAYER_SIZE
        filter_0 = jax.random.normal(k2, (1, field_nums[0] * field_nums[0], field_nums[1]), dtype=jnp.float32) * 0.05
        filter_1 = jax.random.normal(k3, (1, field_nums[0] * field_nums[1], field_nums[2]), dtype=jnp.float32) * 0.05
        return {'inputs': inputs, 'filter_0': filter_0, 'filter_1': filter_1}
    _L0_rec_all = _L0_rec_setup()
    _L0_rec_in = {k: v for k, v in _L0_rec_all.items() if k in ('filter_0', 'filter_1')}
    del _L0_rec_all
    return {'dense_ctx': dense_ctx, 'ids': ids, 'tbl_0': tbl_0, 'tbl_1': tbl_1, 'tbl_2': tbl_2, 'tbl_3': tbl_3, 'tbl_4': tbl_4, 'tbl_5': tbl_5, 'tbl_6': tbl_6, 'tbl_7': tbl_7, 'tbl_8': tbl_8, 'tbl_9': tbl_9, 'tbl_10': tbl_10, 'tbl_11': tbl_11, 'tbl_12': tbl_12, 'tbl_13': tbl_13, 'tbl_14': tbl_14, 'tbl_15': tbl_15, 'tbl_16': tbl_16, 'tbl_17': tbl_17, 'tbl_18': tbl_18, 'tbl_19': tbl_19, 'tbl_20': tbl_20, 'tbl_21': tbl_21, 'tbl_22': tbl_22, 'tbl_23': tbl_23, 'tbl_24': tbl_24, 'tbl_25': tbl_25, 'tbl_26': tbl_26, 'tbl_27': tbl_27, 'tbl_28': tbl_28, 'tbl_29': tbl_29, 'tbl_30': tbl_30, 'tbl_31': tbl_31, 'W_top1': W_top1, 'b_top1': b_top1, 'W_top2': W_top2, 'b_top2': b_top2, 'W_top3': W_top3, 'L0_rec_filter_0': _L0_rec_in['filter_0'], 'L0_rec_filter_1': _L0_rec_in['filter_1']}

def reference(dense_ctx, ids, tbl_0, tbl_1, tbl_2, tbl_3, tbl_4, tbl_5, tbl_6, tbl_7, tbl_8, tbl_9, tbl_10, tbl_11, tbl_12, tbl_13, tbl_14, tbl_15, tbl_16, tbl_17, tbl_18, tbl_19, tbl_20, tbl_21, tbl_22, tbl_23, tbl_24, tbl_25, tbl_26, tbl_27, tbl_28, tbl_29, tbl_30, tbl_31, W_top1, b_top1, W_top2, b_top2, W_top3, L0_rec_filter_0, L0_rec_filter_1):
    import jax
    import jax.numpy as jnp

    def _L0_rec_ref(inputs, filter_0, filter_1):
        import jax, jax.numpy as jnp
        import numpy as np
        B, F, D = (512, 32, 32)
        LAYER_SIZE = [128, 128]

        def _cin_forward(inputs, filters):
            x0 = inputs
            prev = inputs
            outs = []
            for W in filters:
                z = jnp.einsum('bhd,bmd->bhmd', x0, prev)
                b, h, m, d = z.shape
                z = z.reshape(b, h * m, d)
                cur = jnp.einsum('bpd,pn->bnd', z, W[0])
                cur = jax.nn.relu(cur)
                prev = cur
                outs.append(cur)
            result = jnp.concatenate(outs, axis=1)
            return jnp.sum(result, axis=-1)
        return _cin_forward(inputs, (filter_0, filter_1))
    e = jnp.stack([tbl_0[ids[:, 0]], tbl_1[ids[:, 1]], tbl_2[ids[:, 2]], tbl_3[ids[:, 3]], tbl_4[ids[:, 4]], tbl_5[ids[:, 5]], tbl_6[ids[:, 6]], tbl_7[ids[:, 7]], tbl_8[ids[:, 8]], tbl_9[ids[:, 9]], tbl_10[ids[:, 10]], tbl_11[ids[:, 11]], tbl_12[ids[:, 12]], tbl_13[ids[:, 13]], tbl_14[ids[:, 14]], tbl_15[ids[:, 15]], tbl_16[ids[:, 16]], tbl_17[ids[:, 17]], tbl_18[ids[:, 18]], tbl_19[ids[:, 19]], tbl_20[ids[:, 20]], tbl_21[ids[:, 21]], tbl_22[ids[:, 22]], tbl_23[ids[:, 23]], tbl_24[ids[:, 24]], tbl_25[ids[:, 25]], tbl_26[ids[:, 26]], tbl_27[ids[:, 27]], tbl_28[ids[:, 28]], tbl_29[ids[:, 29]], tbl_30[ids[:, 30]], tbl_31[ids[:, 31]]], axis=1)
    z = _L0_rec_ref(e, L0_rec_filter_0, L0_rec_filter_1)
    z = z.reshape(z.shape[0], -1)
    h = jnp.concatenate([z, dense_ctx], axis=1)
    h = jnp.maximum(h @ W_top1 + b_top1, 0.0)
    h = jnp.maximum(h @ W_top2 + b_top2, 0.0)
    y = h @ W_top3
    return y

_drawn_inputs = setup_inputs


def setup_inputs(seed=0):
    import zlib

    import numpy as np

    out = dict(_drawn_inputs(seed))
    spreads = {'b_top1': (0.0, 0.429), 'b_top2': (0.0, 0.415)}
    factors = {'tbl_0': 6.119,
     'tbl_1': 6.096,
     'tbl_2': 6.026,
     'tbl_3': 6.084,
     'tbl_4': 5.856,
     'tbl_5': 6.142,
     'tbl_6': 6.108,
     'tbl_7': 6.222,
     'tbl_8': 6.103,
     'tbl_9': 6.086,
     'tbl_10': 5.887,
     'tbl_11': 5.935,
     'tbl_12': 5.654,
     'tbl_13': 5.961,
     'tbl_14': 6.17,
     'tbl_15': 5.785,
     'tbl_16': 6.316,
     'tbl_17': 6.11,
     'tbl_18': 5.944,
     'tbl_19': 6.376,
     'tbl_20': 5.766,
     'tbl_21': 5.93,
     'tbl_22': 6.134,
     'tbl_23': 5.942,
     'tbl_24': 6.101,
     'tbl_25': 5.65,
     'tbl_26': 5.846,
     'tbl_27': 6.349,
     'tbl_28': 6.2,
     'tbl_29': 6.083,
     'tbl_30': 6.306,
     'tbl_31': 5.691,
     'L0_rec_filter_1': 8.0}
    for name, (base, spread) in spreads.items():
        noise = np.random.default_rng([zlib.crc32(name.encode()), seed]).standard_normal(out[name].shape)
        drawn = base * np.exp(spread * noise) if base else spread * noise
        out[name] = jnp.asarray(drawn.astype(out[name].dtype))
    for name, factor in factors.items():
        out[name] = (out[name] * factor).astype(out[name].dtype)
    return out
```

```python
from contextlib import ExitStack

import concourse.bass as bass
from concourse import mybir

F32 = mybir.dt.float32
F32R = mybir.dt.float32r
I32 = mybir.dt.int32
ALU = mybir.AluOpType
ACT = mybir.ActivationFunctionType
AX_X = mybir.AxisListType.X

P = 128
B = 1024
F = 32
D = 32
N = 128
DQ = 4
COLS = DQ * P
TILES = B // P
PER_TILE = D // DQ
BLOCKS = TILES * PER_TILE
UNITS = 8
CH = 4
HG = F // UNITS
Z_RING = 4
DENSE = 16
H1, H2 = 512, 256

LAYER2_SPLIT = "PDPFPDPF"
PAIR_SPLIT = "DP"
SEL_BASE, SEL_ROT, SEL_REP = 0, 1, 6
N_SEL = SEL_REP + UNITS

F_UNITS = [s for s in range(UNITS) if LAYER2_SPLIT[s] == "F"]


def rank(s, kinds):
    return sum(LAYER2_SPLIT[t] in kinds for t in range(s))


def wait_count(engine, semaphore, count):
    if not (isinstance(count, int) and count <= 0):
        engine.wait_ge(semaphore, count)


def build_program(nc, ids, tables, w1a, w1b, w2, selectors, identity, dense, wt1, wt1d, b1, wt2, b2, wt3, out):
    with ExitStack() as ctx:
        def sb(name, shape, dt=F32):
            return ctx.enter_context(nc.sbuf_tensor(name, shape, dt))

        def sem(name):
            return ctx.enter_context(nc.semaphore(name))

        ids_all = sb("ids_all", [P, TILES, F], I32)
        ids_now = sb("ids_now", [P, 2, F], I32)
        rows = sb("rows", [P, 2, F, D])
        split_rows = sb("split_rows", [P, DQ, P])
        x_pair = sb("x_pair", [P, COLS], F32R)
        x_rep = sb("x_rep", [P, 2, COLS], F32R)
        base = sb("base", [P, COLS])
        pair_z = sb("pair_z", [P, 4, COLS])
        pair_hi = sb("pair_hi", [P, 4, COLS], F32R)
        pair_lo = sb("pair_lo", [P, 4, COLS], F32R)
        last_z = sb("last_z", [P, COLS])
        last_hl = sb("last_hl", [P, COLS], F32R)
        cur = sb("cur", [P, COLS])
        cur_rep = sb("cur_rep", [P, 2, CH, COLS])
        z = sb("z", [P, Z_RING, CH, COLS])
        z_h = sb("z_h", [P, Z_RING - 1, CH, COLS], F32R)
        z_l = sb("z_l", [P, Z_RING - 1, CH, COLS], F32R)
        run1 = sb("run1", [P, DQ, P])
        run2 = sb("run2", [P, DQ, P])
        feat1 = sb("feat1", [P, B])
        feat2 = sb("feat2", [P, B])
        w1_h = sb("w1_h", [P, 5, N], F32R)
        w1_l = sb("w1_l", [P, 5, N], F32R)
        w1_e = sb("w1_e", [P, N], F32R)
        w2_h = sb("w2_h", [P, UNITS * CH, N], F32R)
        w2_l = sb("w2_l", [P, UNITS * CH, N], F32R)
        w2_f = sb("w2_f", [P, max(1, len(F_UNITS)), CH, N])
        sel = sb("sel", [P, N_SEL, P], F32R)
        ident = sb("ident", [P, P])
        b1_sb = sb("b1_sb", [P, H1 // P])
        b2_sb = sb("b2_sb", [P, H2 // P])
        wt3_sb = sb("wt3_sb", [P, H2 // P])
        flat = z[:, :, :, :].rearrange("p a c q -> p (a c q)")
        n2, ns, n1 = UNITS * CH * N, N_SEL * P, 5 * N
        w2_raw = flat[:, 0:n2].rearrange("p (c n) -> p c n", n=N)
        sel_raw = flat[:, n2:n2 + ns].rearrange("p (c n) -> p c n", n=P)
        w1a_raw = flat[:, n2 + ns:n2 + ns + n1].rearrange("p (c n) -> p c n", n=N)
        w1b_raw = flat[:, n2 + ns + n1:n2 + ns + 2 * n1].rearrange("p (c n) -> p c n", n=N)
        h1 = flat[:, 0:4 * B].rearrange("p (c b) -> p c b", c=4)
        h2 = flat[:, 4 * B:6 * B].rearrange("p (c b) -> p c b", c=2)
        y_row = flat[0:1, 6 * B:7 * B]
        crf = cur_rep[:, :, :, :].rearrange("p a c q -> p (a c q)")
        wt1_sb = crf[:, 0:1024].rearrange("p (c n) -> p c n", c=2)
        wt1d_sb = crf[0:DENSE, 1024:1536]
        dense_sb = crf[0:DENSE, 1536:2560]
        wt2_sb = crf[:, 2560:3584].rearrange("p (c n) -> p c n", c=4)

        bank = ctx.enter_context(nc.psum_tensor("bank", [P, 8, COLS], F32))
        ACC2, ACC1, TURN, REP, ROT = 0, 2, 3, 4, 6

        ids_in = sem("ids_in")
        w1_in, w2_in, sel_in, ident_in = sem("w1_in"), sem("w2_in"), sem("sel_in"), sem("ident_in")
        zeros_set = sem("zeros_set")
        sel_ready, w1_summed, w1_hi, w1_ready = sem("sel_ready"), sem("w1_summed"), sem("w1_hi"), sem("w1_ready")
        w2_hi, w2_lo, w2_plain = sem("w2_hi"), sem("w2_lo"), sem("w2_plain")
        ids_copied = sem("ids_copied")
        gathered = [sem("gathered_even"), sem("gathered_odd")]
        staged_hi, staged_lo = sem("staged_hi"), sem("staged_lo")
        turned, x_pair_ready, x_rep_ready = sem("turned"), sem("x_pair_ready"), sem("x_rep_ready")
        base_made, base_ready = sem("base_made"), sem("base_ready")
        rotated, paired = sem("rotated"), sem("paired")
        pair_hi_ready = sem("pair_hi_ready")
        pair_lo_ready = [sem("pair_lo0_ready"), sem("pair_lo1_ready"), sem("pair_lo2_ready")]
        pair_used = sem("pair_used")
        cur_ready, cur_summed, cur_spread = sem("cur_ready"), sem("cur_summed"), sem("cur_spread")
        repeated, z_ready, z_hi_ready = sem("repeated"), sem("z_ready"), sem("z_hi_ready")
        lo_by_dve, lo_by_pool = sem("lo_by_dve"), sem("lo_by_pool")
        z_used, out2_summed = sem("z_used"), sem("out2_summed")
        folded1, folded2 = sem("folded1"), sem("folded2")
        halved1, halved2 = sem("halved1"), sem("halved2")
        top_in, bias_in = sem("top_in"), sem("bias_in")
        top_made, top_act, top_dve, y_out = sem("top_made"), sem("top_act"), sem("top_dve"), sem("y_out")

        block = ctx.enter_context(nc.Block())

        def has(i, inner, ahead):
            return inner or 0 <= i + ahead < BLOCKS

        def run_steps(engine, step, unroll, first, last):
            for i in range(-2, first):
                step(i, i, False)
            with engine.Fori(first // unroll, last // unroll) as q:
                for r in range(unroll):
                    step(q * unroll + r, r, True)
            for i in range(last, BLOCKS):
                step(i, i, False)

        @block.sync
        def _(sp):
            sp.dma_start(ids_all[:], ids).then_inc(ids_in, 16)
            sp.dma_start(sel_raw, selectors).then_inc(sel_in, 16)
            sp.dma_start(ident[:], identity).then_inc(ident_in, 16)
            sp.dma_start(w1a_raw, w1a).then_inc(w1_in, 16)
            sp.dma_start(w1b_raw, w1b).then_inc(w1_in, 16)
            sp.dma_start(w2_raw, w2).then_inc(w2_in, 16)
            sp.dma_start(b1_sb[:], b1).then_inc(bias_in, 16)
            sp.dma_start(b2_sb[:], b2).then_inc(bias_in, 16)
            sp.dma_start(wt3_sb[:], wt3).then_inc(bias_in, 16)

            def spread(k, parity):
                sp.wait_ge(cur_ready, k + 1)
                for c in range(CH):
                    for j in range(4):
                        sp.dma_start(cur_rep[32 * j:32 * j + 32, parity, c, :],
                                     cur[32 * c:32 * c + 32, :]).then_inc(cur_spread, 16)

            for k in range(4):
                spread(k, k % 2)
            with sp.Fori(2, BLOCKS // 2) as q:
                for r in range(2):
                    spread(q * 2 + r, r)

            sp.wait_ge(z_ready, UNITS * BLOCKS)
            sp.dma_start(wt1_sb, wt1).then_inc(top_in, 16)
            sp.dma_start(wt1d_sb, wt1d).then_inc(top_in, 16)
            sp.dma_start(dense_sb, dense).then_inc(top_in, 16)
            sp.dma_start(wt2_sb, wt2).then_inc(top_in, 16)
            sp.wait_ge(top_act, 2 * 3 + 1)
            sp.wait_ge(top_dve, 2 * 3 + 1)
            sp.dma_start(out, y_row).then_inc(y_out, 16)
            sp.wait_ge(y_out, 16)

        @block.gpsimd
        def _(pool):
            pool.wait_ge(ids_in, 16)

            def take_ids(t, parity):
                pool.tensor_copy(ids_now[:, parity, :], ids_all[:, t, :] if isinstance(t, int)
                                 else ids_all[:, bass.ds(t, 1), :]).then_inc(ids_copied, 1)
                pool.wait_ge(ids_copied, t + 1)

            def gather(f, parity):
                pool.indirect_dma_start(rows[:, parity, f, :], None, tables[f],
                                        bass.IndirectOffsetOnAxis(ids_now[:, parity, f:f + 1], 0)
                                        ).then_inc(gathered[parity], 16)

            take_ids(0, 0)
            for f in range(F):
                gather(f, 0)

            def pair_low(i, inner, g):
                if PAIR_SPLIT[g] == "P" and has(i, inner, 1):
                    pool.wait_ge(pair_hi_ready, 3 * (i + 1) + g + 1)
                    pool.tensor_tensor(pair_lo[:, 2 * g:2 * g + 2, :], pair_z[:, 2 * g:2 * g + 2, :],
                                       pair_hi[:, 2 * g:2 * g + 2, :].bitcast(F32), ALU.subtract
                                       ).then_inc(pair_lo_ready[g], 1)

            def step(i, r, inner):
                tile_ahead = (r + 10) // PER_TILE
                t = i + (PER_TILE * tile_ahead - r) if isinstance(i, int) else None
                parity, group = tile_ahead % 2, (r + 2) % PER_TILE
                fetch = inner or tile_ahead < TILES
                if inner:
                    t = (i - r) // PER_TILE + tile_ahead
                else:
                    t = tile_ahead
                if fetch and group == 0:
                    wait_count(pool, staged_lo, PER_TILE * (t - 1))
                    wait_count(pool, gathered[parity], 16 * F * (t // 2) if isinstance(t, int)
                               else 8 * F * (t - parity))
                    pool.wait_ge(ids_in, 16)
                    take_ids(t, parity)
                pair_low(i, inner, 0)
                for s in range(UNITS):
                    if LAYER2_SPLIT[s] == "P" and has(i, inner, 0):
                        n_hi = rank(UNITS, "PD") * i + rank(s, "PD") + 1
                        pool.wait_ge(z_hi_ready, n_hi)
                        pool.tensor_tensor(z_l[:, s % Z_RING], z[:, s % Z_RING],
                                           z_h[:, s % Z_RING].bitcast(F32), ALU.subtract
                                           ).then_inc(lo_by_pool, 1)
                    if s == 0:
                        pair_low(i, inner, 1)
                    if s in (1, 3, 5, 7) and fetch:
                        gather(4 * group + s // 2, parity)

            run_steps(pool, step, 16, 16, 48)

        @block.scalar
        def _(act):
            act.wait_ge(sel_in, 16)
            act.activation(sel[:], sel_raw, ACT.Copy).then_inc(sel_ready, 1)
            act.wait_ge(w1_summed, 1)
            act.activation(w1_h[:], w1a_raw, ACT.Copy).then_inc(w1_hi, 1)
            act.wait_ge(w2_in, 16)
            act.activation(w2_h[:], w2_raw, ACT.Copy).then_inc(w2_hi, 1)

            def pair_high(i, inner, g):
                if has(i, inner, 1):
                    n = 3 * (i + 1) + g
                    if g < 2:
                        act.wait_ge(paired, 5 * (i + 1) + 2 * g + 2)
                        act.activation(pair_hi[:, 2 * g:2 * g + 2, :], pair_z[:, 2 * g:2 * g + 2, :],
                                       ACT.Copy).then_inc(pair_hi_ready, 1)
                    else:
                        act.wait_ge(paired, 5 * (i + 1) + 5)
                        act.activation(last_hl[:], last_z[:], ACT.Copy).then_inc(pair_hi_ready, 1)

            def step(i, r, inner):
                k2, tile2 = r + 2, (r + 2) // PER_TILE
                pair_high(i, inner, 0)
                for s in range(UNITS):
                    if LAYER2_SPLIT[s] != "F" and has(i, inner, 0):
                        act.wait_ge(z_ready, UNITS * i + s + 1)
                        act.activation(z_h[:, s % Z_RING], z[:, s % Z_RING], ACT.Copy).then_inc(z_hi_ready, 1)
                    if s == 0:
                        pair_high(i, inner, 1)
                    if s == 1:
                        pair_high(i, inner, 2)
                        if has(i, inner, 2):
                            n_tile = (i + 2 - (r + 2) % PER_TILE) // PER_TILE if isinstance(i, int) else None
                            if n_tile is not None:
                                act.wait_ge(gathered[tile2 % 2], 16 * F * (n_tile // 2 + 1))
                            else:
                                act.wait_ge(gathered[tile2 % 2], (i - r) * F + 16 * F * (tile2 // 2 + 1))
                            if not isinstance(i, int) or i + 2 >= 1:
                                act.wait_ge(turned, i + 2)
                            else:
                                act.wait_ge(zeros_set, 1)
                            d0 = DQ * (k2 % PER_TILE)
                            act.activation(split_rows[:, :, 0:F].bitcast(F32R),
                                           rows[:, tile2 % 2, :, d0:d0 + DQ].rearrange("p f d -> p d f"),
                                           ACT.Copy).then_inc(staged_hi, 1)
                    if s == 3 and has(i, inner, 1):
                        act.wait_ge(pair_used, 3 * (i + 1) + 3)
                        wait_count(act, cur_spread, 16 * 16 * (i + 1))
                        wait_count(act, cur_summed, i + 1)
                        act.activation(cur[:], bank[:, ACC1, :], ACT.Relu).then_inc(cur_ready, 1)
                    if s == 3 and has(i, inner, 2):
                        act.wait_ge(turned, i + 3)
                        act.activation(x_pair[:], bank[:, TURN, :], ACT.Copy).then_inc(x_pair_ready, 1)
                    if s == 4 and has(i, inner, 2):
                        act.wait_ge(base_made, i + 3)
                        wait_count(act, paired, 5 * (i + 2))
                        act.activation(base[:], bank[:, TURN, :], ACT.Copy).then_inc(base_ready, 1)
                if has(i, inner, 2):
                    wait_count(act, repeated, UNITS * (i + 1))
                    act.wait_ge(x_pair_ready, i + 3)
                    act.activation(x_rep[:, r % 2, :], x_pair[:].bitcast(F32), ACT.Copy).then_inc(x_rep_ready, 1)

            run_steps(act, step, 16, 16, 48)

            act.wait_ge(bias_in, 48)
            for n in range(4):
                act.wait_ge(top_made, n + 1)
                act.activation(h1[:, n, 0:COLS], bank[:, n, :], ACT.Relu, bias=b1_sb[:, n:n + 1]).then_inc(top_act, 1)
            for n in range(2):
                act.wait_ge(top_made, 8 + n + 1)
                act.activation(h2[:, n, 0:COLS], bank[:, n, :], ACT.Relu, bias=b2_sb[:, n:n + 1]).then_inc(top_act, 1)
            act.wait_ge(top_made, 13)
            act.activation(y_row[:, 0:COLS], bank[0:1, 4, :], ACT.Copy).then_inc(top_act, 1)

        @block.vector
        def _(dve):
            dve.memset(split_rows[:], 0.0).then_inc(zeros_set, 1)
            dve.wait_ge(w1_in, 32)
            dve.tensor_tensor(w1a_raw, w1a_raw, w1b_raw, ALU.add).then_inc(w1_summed, 1)
            dve.wait_ge(w1_hi, 1)
            dve.wait_ge(w1_summed, 1)
            dve.tensor_tensor(w1_l[:], w1a_raw, w1_h[:].bitcast(F32), ALU.subtract).then_inc(w1_ready, 1)
            dve.tensor_copy(w1_e[:], w1_h[:, 4, :].bitcast(F32)).then_inc(w1_ready, 1)
            dve.wait_ge(w1_ready, 2)
            dve.tensor_copy(w1_e[0:32, :], w1_l[0:32, 4, :].bitcast(F32)).then_inc(w1_ready, 1)
            dve.wait_ge(w1_ready, 3)
            dve.tensor_copy(w1_e[0:16, :], w1_h[0:16, 4, :].bitcast(F32)).then_inc(w1_ready, 1)
            dve.wait_ge(w2_hi, 1)
            dve.tensor_tensor(w2_l[:], w2_raw, w2_h[:].bitcast(F32), ALU.subtract).then_inc(w2_lo, 1)
            for n, s in enumerate(F_UNITS):
                dve.tensor_copy(w2_f[:, n], w2_raw[:, CH * s:CH * s + CH, :]).then_inc(w2_plain, 1)
            dve.wait_ge(sel_ready, 1)
            dve.wait_ge(w2_lo, 1)
            if F_UNITS:
                dve.wait_ge(w2_plain, len(F_UNITS))

            def pair_mul(i, inner, ahead, tiles, r):
                if not has(i, inner, ahead):
                    return
                for a in tiles:
                    n = 5 * (i + ahead) + a
                    dve.wait_ge(rotated, n + 1)
                    if a == 0:
                        dve.wait_ge(base_ready, i + ahead + 1)
                    g = a // 2
                    wait_count(dve, pair_used, 3 * (i + ahead - 1) + g + 1)
                    o = last_z[:] if a == 4 else pair_z[:, a, :]
                    dve.tensor_tensor(o, bank[:, ROT + (r + ahead + a) % 2, :], base[:], ALU.mult).then_inc(paired, 1)

            def pair_low(i, inner, g):
                if g < 2 and PAIR_SPLIT[g] != "D" or not has(i, inner, 1):
                    return
                dve.wait_ge(pair_hi_ready, 3 * (i + 1) + g + 1)
                if g < 2:
                    dve.tensor_tensor(pair_lo[:, 2 * g:2 * g + 2, :], pair_z[:, 2 * g:2 * g + 2, :],
                                      pair_hi[:, 2 * g:2 * g + 2, :].bitcast(F32), ALU.subtract
                                      ).then_inc(pair_lo_ready[g], 1)
                else:
                    dve.tensor_tensor(last_hl[32:64, :], last_z[32:64, :], last_hl[32:64, :].bitcast(F32),
                                      ALU.subtract).then_inc(pair_lo_ready[2], 1)

            def low(i, s):
                if LAYER2_SPLIT[s] == "D":
                    dve.wait_ge(z_hi_ready, rank(UNITS, "PD") * i + rank(s, "PD") + 1)
                    dve.tensor_tensor(z_l[:, s % Z_RING], z[:, s % Z_RING], z_h[:, s % Z_RING].bitcast(F32),
                                      ALU.subtract).then_inc(lo_by_dve, 1)

            def add_relu(run, source, k, first, done):
                flat_run = run[:].rearrange("p d b -> p (d b)")
                if first:
                    dve.tensor_scalar(flat_run, source, 0.0, None, ALU.max).then_inc(done, 1)
                else:
                    dve.wait_ge(done, k)
                    dve.scalar_tensor_tensor(flat_run, source, 0.0, flat_run, ALU.max, ALU.add).then_inc(done, 1)

            def sum2(i, r, inner):
                if not has(i, inner, -1):
                    return
                dve.wait_ge(z_used, UNITS * i)
                rk = (r - 1) % 16 if inner else r - 1
                kk = i - 1
                if rk % PER_TILE == 0:
                    wait_count(dve, folded2, fold_count(i, r, inner, -1))
                add_relu(run2, bank[:, ACC2 + rk % 2, :], kk, rk % PER_TILE == 0, out2_summed)
                if rk % PER_TILE == PER_TILE - 1:
                    fold2(i, r, inner, -1, run2, feat2, out2_summed, folded2)

            def fold_count(i, r, inner, ahead):
                if not inner:
                    return (i + ahead) // PER_TILE
                return (i - r) // PER_TILE + (r + ahead) // PER_TILE

            def fold2(i, r, inner, ahead, run, feat, done_sum, folded):
                halved, halves = (halved1 if run is run1 else halved2), fold_count(i, r, inner, ahead) + 1
                dve.wait_ge(done_sum, i + ahead + 1)
                if not inner:
                    t = (i + ahead) // PER_TILE
                    o = feat[:, P * t:P * t + P]
                else:
                    o = feat[:, bass.ds((i - r) * (P // PER_TILE) + P * ((r + ahead) // PER_TILE), P)]
                dve.tensor_tensor(run[:, 0:2, :], run[:, 0:2, :], run[:, 2:4, :], ALU.add).then_inc(halved, 1)
                dve.wait_ge(halved, halves)
                dve.tensor_tensor(o, run[:, 0, :], run[:, 1, :], ALU.add).then_inc(folded, 1)

            def step(i, r, inner):
                for s in range(UNITS):
                    if has(i, inner, 0):
                        n = UNITS * i + s
                        dve.wait_ge(repeated, n + 1)
                        wait_count(dve, z_used, n - Z_RING + 1)
                        if s == 0:
                            dve.wait_ge(cur_spread, 16 * 16 * (i + 1))
                        dve.tensor_tensor(z[:, s % Z_RING],
                                          bank[:, REP + s % 2, :].unsqueeze(1).to_broadcast([P, CH, COLS]),
                                          cur_rep[:, r % 2, :, :], ALU.mult).then_inc(z_ready, 1)
                        if s:
                            low(i, s - 1)
                    if s == 0:
                        if has(i, inner, -1):
                            low(i - 1, UNITS - 1)
                        pair_mul(i, inner, 1, (2, 3), r)
                        pair_low(i, inner, 0)
                    if s == 1:
                        pair_mul(i, inner, 1, (4,), r)
                        pair_low(i, inner, 1)
                    if s == 2:
                        pair_low(i, inner, 2)
                        if has(i, inner, 2):
                            dve.wait_ge(staged_hi, i + 3)
                            k2 = r + 2
                            d0 = DQ * (k2 % PER_TILE)
                            dve.tensor_tensor(split_rows[:, :, F:2 * F],
                                              rows[:, (k2 // PER_TILE) % 2, :, d0:d0 + DQ].rearrange("p f d -> p d f"),
                                              split_rows[:, :, 0:F], ALU.subtract).then_inc(staged_lo, 1)
                    if s == 3:
                        sum2(i, r, inner)
                    if s == 4 and has(i, inner, 1):
                        k1 = r + 1
                        dve.wait_ge(cur_ready, i + 2)
                        if k1 % PER_TILE == 0:
                            wait_count(dve, folded1, fold_count(i, r, inner, 1))
                        add_relu(run1, cur[:], i + 1, k1 % PER_TILE == 0, cur_summed)
                        if k1 % PER_TILE == PER_TILE - 1:
                            fold2(i, r, inner, 1, run1, feat1, cur_summed, folded1)
                    if s == UNITS - 1:
                        pair_mul(i, inner, 2, (0, 1), r)

            run_steps(dve, step, 16, 16, 48)
            low(BLOCKS - 1, UNITS - 1)
            sum2(BLOCKS, BLOCKS, False)

            dve.wait_ge(bias_in, 48)
            for n in range(4):
                dve.wait_ge(top_made, 4 + n + 1)
                dve.tensor_scalar(h1[:, n, COLS:B], bank[:, 4 + n, :], b1_sb[:, n:n + 1], 0.0,
                                  ALU.add, ALU.max).then_inc(top_dve, 1)
            for n in range(2):
                dve.wait_ge(top_made, 10 + n + 1)
                dve.tensor_scalar(h2[:, n, COLS:B], bank[:, 2 + n, :], b2_sb[:, n:n + 1], 0.0,
                                  ALU.add, ALU.max).then_inc(top_dve, 1)
            dve.wait_ge(top_made, 14)
            dve.tensor_copy(y_row[:, COLS:B], bank[0:1, 5, :]).then_inc(top_dve, 1)

        @block.tensor
        def _(pe):
            pe.wait_ge(sel_ready, 1)
            pe.wait_ge(ident_in, 16)

            def repeat_fields(i, inner, ahead, s, parity):
                if has(i, inner, ahead):
                    n = UNITS * (i + ahead) + s
                    if s == 0:
                        pe.wait_ge(x_rep_ready, i + ahead + 1)
                    wait_count(pe, z_ready, n - 1)
                    pe.matmul(bank[:, REP + s % 2, :], sel[:, SEL_REP + s, :], x_rep[:, parity, :],
                              start=True, stop=True).then_inc(repeated, 1)

            def rotate(i, inner, tiles, parity):
                if has(i, inner, 2):
                    for a in tiles:
                        wait_count(pe, paired, 5 * (i + 2) + a - 1)
                        pe.matmul(bank[:, ROT + (parity + a) % 2, :], sel[:, SEL_ROT + a, :], x_pair[:],
                                  start=True, stop=True).then_inc(rotated, 1)

            def split_product(acc, wh, wl, hi, lo, start, stop):
                pe.matmul(acc, wh, hi, start=start, stop=False)
                pe.matmul(acc, wl, hi, start=False, stop=False)
                return pe.matmul(acc, wh, lo, start=False, stop=stop)

            def pair_products(i, inner, ahead, g):
                if not has(i, inner, ahead):
                    return
                k = i + ahead
                acc = bank[:, ACC1, :]
                if g == 0:
                    wait_count(pe, cur_ready, k)
                    if isinstance(k, int) and k == 0:
                        pe.wait_ge(w1_ready, 4)
                pe.wait_ge(pair_hi_ready, 3 * k + g + 1)
                pe.wait_ge(pair_lo_ready[g], k + 1)
                if g < 2:
                    for a in (2 * g, 2 * g + 1):
                        mm = split_product(acc, w1_h[:, a, :], w1_l[:, a, :], pair_hi[:, a, :], pair_lo[:, a, :],
                                           a == 0, False)
                else:
                    mm = pe.matmul(acc, w1_e[:], last_hl[:], start=False, stop=True)
                mm.then_inc(pair_used, 1)

            def unit_products(i, s, parity, between):
                acc = bank[:, ACC2 + parity, :]
                if s == 0:
                    wait_count(pe, out2_summed, i - 1)
                    if isinstance(i, int) and i == 0:
                        pe.wait_ge(w2_lo, 1)
                        if F_UNITS:
                            pe.wait_ge(w2_plain, len(F_UNITS))
                kind = LAYER2_SPLIT[s]
                if kind == "F":
                    pe.wait_ge(z_ready, UNITS * i + s + 1)
                elif kind == "D":
                    pe.wait_ge(lo_by_dve, rank(UNITS, "D") * i + rank(s, "D") + 1)
                else:
                    pe.wait_ge(lo_by_pool, rank(UNITS, "P") * i + rank(s, "P") + 1)
                for c in range(CH):
                    if c == 2:
                        between()
                    ch = CH * s + c
                    start, stop = s == 0 and c == 0, s == UNITS - 1 and c == CH - 1
                    if kind == "F":
                        mm = pe.matmul(acc, w2_f[:, F_UNITS.index(s), c, :], z[:, s % Z_RING, c, :],
                                       start=start, stop=stop)
                    else:
                        mm = split_product(acc, w2_h[:, ch, :], w2_l[:, ch, :], z_h[:, s % Z_RING, c, :],
                                           z_l[:, s % Z_RING, c, :], start, stop)
                mm.then_inc(z_used, 1)

            def step(i, r, inner):
                parity = r % 2
                for s in range(UNITS):
                    if s == 1 and has(i, inner, 2):
                        pe.wait_ge(staged_lo, i + 3)
                        wait_count(pe, base_ready, i + 2)
                        for d in range(DQ):
                            mm = pe.transpose(bank[:, TURN, P * d:P * d + P], split_rows[:, d, :], ident[:])
                        mm.then_inc(turned, 1)
                    if s + 3 < UNITS:
                        repeat_fields(i, inner, 0, s + 3, parity)
                    else:
                        repeat_fields(i, inner, 1, s + 3 - UNITS, 1 - parity)
                    if s == 2 and has(i, inner, 2):
                        pe.wait_ge(x_pair_ready, i + 3)
                        pe.matmul(bank[:, TURN, :], sel[:, SEL_BASE, :], x_pair[:], start=True, stop=True
                                  ).then_inc(base_made, 1)
                    if s == 4:
                        rotate(i, inner, (0, 1), parity)

                    def between():
                        if s == 5:
                            rotate(i, inner, (2, 3), parity)
                        if s == 6:
                            rotate(i, inner, (4,), parity)

                    if has(i, inner, 0):
                        unit_products(i, s, parity, between)
                    else:
                        between()
                    if s == 0:
                        pair_products(i, inner, 1, 1)
                        pair_products(i, inner, 1, 2)
                    if s == 7:
                        pair_products(i, inner, 2, 0)

            run_steps(pe, step, 2, 2, BLOCKS - 2)

            pe.wait_ge(top_in, 64)
            pe.wait_ge(bias_in, 48)
            pe.wait_ge(folded1, TILES)
            pe.wait_ge(folded2, TILES)
            for half in range(2):
                cols = slice(COLS * half, COLS * half + COLS)
                for n in range(4):
                    acc, m = bank[:, 4 * half + n, :], slice(P * n, P * n + P)
                    pe.matmul(acc, wt1_sb[:, 0, m], feat1[:, cols], start=True, stop=False)
                    pe.matmul(acc, wt1_sb[:, 1, m], feat2[:, cols], start=False, stop=False)
                    pe.matmul(acc, wt1d_sb[:, m], dense_sb[:, cols], start=False, stop=True).then_inc(top_made, 1)
            for half, done in ((0, top_act), (1, top_dve)):
                pe.wait_ge(done, 4)
                if half:
                    pe.wait_ge(top_act, 4)
                cols = slice(COLS * half, COLS * half + COLS)
                for n in range(2):
                    acc = bank[:, 2 * half + n, :]
                    for c in range(4):
                        mm = pe.matmul(acc, wt2_sb[:, c, P * n:P * n + P], h1[:, c, cols], start=(c == 0), stop=(c == 3))
                    mm.then_inc(top_made, 1)
            for half, done in ((0, top_act), (1, top_dve)):
                pe.wait_ge(done, 6)
                for c in range(2):
                    mm = pe.matmul(bank[0:1, 4 + half, :], wt3_sb[:, c:c + 1], h2[:, c, COLS * half:COLS * half + COLS],
                                   start=(c == 0), stop=(c == 1))
                mm.then_inc(top_made, 1)


def layouts():
    import numpy as np
    r = np.arange(P)
    kk, m = r // 32, r % 32
    first = np.zeros((P, 5), np.int64)
    second = np.zeros((P, 5), np.int64)
    for a in range(4):
        other = (m + 4 * a + kk) % F
        first[:, a], second[:, a] = m * F + other, other * F + m
    m16 = r % 16
    first[:, 4], second[:, 4] = m16 * F + m16 + 16, (m16 + 16) * F + m16
    sel = np.zeros((P, N_SEL, P), np.float32)
    for half in (0, 32):
        sel[half + m, SEL_BASE, r] = 1.0
        for a in range(4):
            sel[half + (m + 4 * a + kk) % F, SEL_ROT + a, r] = 1.0
        sel[half + (m + 16) % F, SEL_ROT + 4, r] = 1.0
        for s in range(UNITS):
            sel[half + HG * s + kk, SEL_REP + s, r] = 1.0
    return first, second, sel, np.eye(P, dtype=np.float32)


def kernel(**inputs):
    import numpy as np
    import concourse.bacc as bacc
    from concourse.bass_utils import run_bass_kernel_spmd

    first, second, sel, eye = layouts()
    f0 = np.asarray(inputs["L0_rec_filter_0"])[0]
    f1 = np.asarray(inputs["L0_rec_filter_1"])[0]
    w1a = f0[first]
    w1b = f0[second]
    w1b[:F, 0] = 0
    w1a[48:, 4] = 0
    w1b[48:, 4] = 0
    w2 = f1.reshape(UNITS, HG, CH, 32, N).transpose(1, 3, 0, 2, 4).reshape(P, UNITS * CH, N)
    wt1 = np.asarray(inputs["W_top1"])
    arrays = {
        "ids": np.asarray(inputs["ids"]).reshape(TILES, P, F).transpose(1, 0, 2),
        **{f"tbl_{f}": np.asarray(inputs[f"tbl_{f}"]) for f in range(F)},
        "w1a": w1a, "w1b": w1b, "w2": w2, "selectors": sel, "identity": eye,
        "dense": np.asarray(inputs["dense_ctx"]).T,
        "wt1": wt1[:2 * N].reshape(2, P, H1).transpose(1, 0, 2),
        "wt1d": wt1[2 * N:],
        "b1": np.asarray(inputs["b_top1"]).reshape(H1 // P, P).T,
        "wt2": np.asarray(inputs["W_top2"]).reshape(4, P, H2).transpose(1, 0, 2),
        "b2": np.asarray(inputs["b_top2"]).reshape(H2 // P, P).T,
        "wt3": np.asarray(inputs["W_top3"]).reshape(H2 // P, P).T,
    }
    arrays = {name: np.ascontiguousarray(a) for name, a in arrays.items()}
    nc = bacc.Bacc("TRN2", target_bir_lowering=False, num_devices=1)
    ap = {name: nc.dram_tensor(name, a.shape, mybir.dt.from_np(a.dtype), kind="ExternalInput").ap()
          for name, a in arrays.items()}
    y = nc.dram_tensor("y", (1, B), F32, kind="ExternalOutput").ap()
    build_program(nc, ap["ids"], [ap[f"tbl_{f}"] for f in range(F)], ap["w1a"], ap["w1b"], ap["w2"], ap["selectors"],
                  ap["identity"], ap["dense"], ap["wt1"], ap["wt1d"], ap["b1"], ap["wt2"], ap["b2"], ap["wt3"], y)
    r = run_bass_kernel_spmd(nc, [arrays], core_ids=[0])
    return r.results[0]["y"].reshape(B, 1)
```

```python
from contextlib import ExitStack

import concourse.bass as bass
from concourse import mybir

F32 = mybir.dt.float32
F32R = mybir.dt.float32r
I32 = mybir.dt.int32
ALU = mybir.AluOpType
ACT = mybir.ActivationFunctionType
AX_X = mybir.AxisListType.X

P = 128
B = 1024
F = 32
D = 32
N = 128
DQ = 4
COLS = DQ * P
TILES = B // P
PER_TILE = D // DQ
BLOCKS = TILES * PER_TILE
GROUP = 4
GROUPS = F // GROUP // 2
QUARTERS = GROUPS * DQ
DENSE = 16
H1, H2 = 512, 256

GATHER_AT = (2, 6, 10, 14)
PAIR_SPLIT = "DP"
SEL_BASE, SEL_ROT = 0, 1
N_SEL = 6


def wait_count(engine, semaphore, count):
    if not (isinstance(count, int) and count <= 0):
        engine.wait_ge(semaphore, count)


def build_program(nc, ids, tables, w1a, w1b, w2, selectors, identity, dense, wt1, wt1d, b1, wt2, b2, wt3, out):
    with ExitStack() as ctx:
        def sb(name, shape, dt=F32):
            return ctx.enter_context(nc.sbuf_tensor(name, shape, dt))

        def sem(name):
            return ctx.enter_context(nc.semaphore(name))

        ids_all = sb("ids_all", [P, TILES, F], I32)
        ids_now = sb("ids_now", [P, 2, F], I32)
        rows = sb("rows", [P, 2, F, D])
        split_rows = sb("split_rows", [P, DQ, P], F32R)
        x_pair = sb("x_pair", [P, COLS], F32R)
        x_rows = sb("x_rows", [P, 8, F, DQ])
        base = sb("base", [P, COLS])
        pair_z = sb("pair_z", [P, 4, COLS])
        pair_hi = sb("pair_hi", [P, 4, COLS], F32R)
        pair_lo = sb("pair_lo", [P, 4, COLS], F32R)
        last_hl = sb("last_hl", [P, COLS], F32R)
        cur = sb("cur", [P, 2, COLS])
        cur_h = sb("cur_h", [P, 2, DQ, P], F32R)
        cur_l = sb("cur_l", [P, 2, DQ, P], F32R)
        work = sb("work", [P, 7 * B])
        scaled_sum = sb("scaled_sum", [P, 2, COLS])
        halves = sb("halves", [P, DQ, 2, N])
        out2 = sb("out2", [P, DQ, N])
        run1 = sb("run1", [P, DQ, P])
        run2 = sb("run2", [P, DQ, P])
        feat2_rows = sb("feat2_rows", [P, TILES, N])
        feat1 = sb("feat1", [P, B])
        feat2 = sb("feat2", [P, B])
        w1_h = sb("w1_h", [P, 4, N], F32R)
        w1_l = sb("w1_l", [P, 4, N], F32R)
        w1_e = sb("w1_e", [P, N], F32R)
        w2_h = sb("w2_h", [P, F, N], F32R)
        w2_l = sb("w2_l", [P, F, N], F32R)
        sel = sb("sel", [P, N_SEL, P], F32R)
        ident = sb("ident", [P, P], F32R)
        b1_sb = sb("b1_sb", [P, H1 // P])
        b2_sb = sb("b2_sb", [P, H2 // P])
        wt3_sb = sb("wt3_sb", [P, H2 // P])
        wt1_sb = sb("wt1_sb", [P, 2, H1])
        wt1d_sb = sb("wt1d_sb", [DENSE, H1])
        dense_sb = sb("dense_sb", [DENSE, B])
        wt2_sb = sb("wt2_sb", [P, 4, H2])
        ns, n1 = N_SEL * P, 5 * N
        w2_raw = work[:, 0:F * N].rearrange("p (c n) -> p c n", n=N)
        at = F * N
        sel_raw = work[:, at:at + ns].rearrange("p (c n) -> p c n", n=P)
        w1a_raw = work[:, at + ns:at + ns + n1].rearrange("p (c n) -> p c n", n=N)
        w1b_raw = work[:, at + ns + n1:at + ns + 2 * n1].rearrange("p (c n) -> p c n", n=N)
        ident_raw = work[:, at + ns + 2 * n1:at + ns + 2 * n1 + P]
        scaled = work[:, 0:4 * B].rearrange("p (a g n) -> p a g n", a=2, g=GROUPS)
        chain = work[:, 4 * B:6 * B].rearrange("p (d j n) -> p d j n", d=DQ, j=GROUP)
        partial = work[:, 6 * B:7 * B].rearrange("p (a n) -> p a n", a=2)
        h1 = work[:, 0:4 * B].rearrange("p (c b) -> p c b", c=4)
        h2 = work[:, 4 * B:6 * B].rearrange("p (c b) -> p c b", c=2)
        y_row = work[0:1, 6 * B:7 * B]

        bank = ctx.enter_context(nc.psum_tensor("bank", [P, 8, COLS], F32))
        U_SCALED, U_CHAINED, ACC1, TURN, ROT = 0, 2, 4, 5, 6

        ids_in = sem("ids_in")
        w1_in, w2_in, sel_in, ident_in = sem("w1_in"), sem("w2_in"), sem("sel_in"), sem("ident_in")
        zeros_set = sem("zeros_set")
        sel_ready, w1_summed, w1_hi, w1_ready = sem("sel_ready"), sem("w1_summed"), sem("w1_hi"), sem("w1_ready")
        w2_hi, w2_lo = sem("w2_hi"), sem("w2_lo")
        ids_copied = sem("ids_copied")
        gathered = [sem("gathered_even"), sem("gathered_odd")]
        staged_hi, staged_lo = sem("staged_hi"), sem("staged_lo")
        turned, x_pair_ready, x_rows_ready = sem("turned"), sem("x_pair_ready"), sem("x_rows_ready")
        base_made, base_ready = sem("base_made"), sem("base_ready")
        rotated, paired = sem("rotated"), sem("paired")
        pair_hi_ready = sem("pair_hi_ready")
        pair_lo_ready = [sem("pair_lo0_ready"), sem("pair_lo1_ready"), sem("pair_lo2_ready")]
        pair_used = sem("pair_used")
        cur_ready, cur_hi_ready, cur_lo_ready, cur_summed = sem("cur_ready"), sem("cur_hi_ready"), sem("cur_lo_ready"), sem("cur_summed")
        u_scaled_made, u_chained_made = sem("u_scaled_made"), sem("u_chained_made")
        group_scaled, partial_made, scaled_summed = sem("group_scaled"), sem("partial_made"), sem("scaled_summed")
        chained, chains_halved, out2_made, out2_summed = sem("chained"), sem("chains_halved"), sem("out2_made"), sem("out2_summed")
        rows_turned, feat2_ready = sem("rows_turned"), sem("feat2_ready")
        folded1, folded2 = sem("folded1"), sem("folded2")
        halved1, halved2, cleared1 = sem("halved1"), sem("halved2"), sem("cleared1")
        top_in, bias_in = sem("top_in"), sem("bias_in")
        top_made, top_act, top_dve, y_out = sem("top_made"), sem("top_act"), sem("top_dve"), sem("y_out")

        block = ctx.enter_context(nc.Block())

        def has(i, inner, ahead):
            return inner or 0 <= i + ahead < BLOCKS

        def run_steps(engine, step, unroll, first, last):
            for i in range(-3, first):
                step(i, i, False)
            with engine.Fori(first // unroll, last // unroll) as q:
                for r in range(unroll):
                    step(q * unroll + r, r, True)
            for i in range(last, BLOCKS + 1):
                step(i, i, False)

        @block.sync
        def _(sp):
            sp.dma_start(ids_all[:], ids).then_inc(ids_in, 16)
            sp.dma_start(sel_raw, selectors).then_inc(sel_in, 16)
            sp.dma_start(ident_raw, identity).then_inc(ident_in, 16)
            sp.dma_start(w1a_raw, w1a).then_inc(w1_in, 16)
            sp.dma_start(w1b_raw, w1b).then_inc(w1_in, 16)
            sp.dma_start(w2_raw, w2).then_inc(w2_in, 16)
            sp.dma_start(b1_sb[:], b1).then_inc(bias_in, 16)
            sp.dma_start(b2_sb[:], b2).then_inc(bias_in, 16)
            sp.dma_start(wt3_sb[:], wt3).then_inc(bias_in, 16)

            sp.dma_start(wt1_sb[:], wt1).then_inc(top_in, 16)
            sp.dma_start(wt1d_sb[:], wt1d).then_inc(top_in, 16)
            sp.dma_start(dense_sb[:], dense).then_inc(top_in, 16)
            sp.dma_start(wt2_sb[:], wt2).then_inc(top_in, 16)
            sp.wait_ge(top_act, 2 * 3 + 1)
            sp.wait_ge(top_dve, 2 * 3 + 1)
            sp.dma_start(out, y_row).then_inc(y_out, 16)
            sp.wait_ge(y_out, 16)

        @block.gpsimd
        def _(pool):
            pool.wait_ge(ids_in, 16)

            def take_ids(t, parity):
                pool.tensor_copy(ids_now[:, parity, :], ids_all[:, t, :] if isinstance(t, int)
                                 else ids_all[:, bass.ds(t, 1), :]).then_inc(ids_copied, 1)
                pool.wait_ge(ids_copied, t + 1)

            def gather(f, parity):
                pool.indirect_dma_start(rows[:, parity, f, :], None, tables[f],
                                        bass.IndirectOffsetOnAxis(ids_now[:, parity, f:f + 1], 0)
                                        ).then_inc(gathered[parity], 16)

            take_ids(0, 0)
            for f in range(F):
                gather(f, 0)

            def pair_low(i, inner, g, ahead):
                if PAIR_SPLIT[g] == "P" and has(i, inner, ahead):
                    pool.wait_ge(pair_hi_ready, 3 * (i + ahead) + g + 1)
                    pool.tensor_tensor(pair_lo[:, 2 * g:2 * g + 2, :], pair_z[:, 2 * g:2 * g + 2, :],
                                       pair_hi[:, 2 * g:2 * g + 2, :].bitcast(F32), ALU.subtract
                                       ).then_inc(pair_lo_ready[g], 1)

            def sum_scaled(k, d):
                n = DQ * k + d
                pool.wait_ge(group_scaled, GROUPS * (n + 1))
                wait_count(pool, scaled_summed, n)
                pool.tensor_tensor(partial, scaled[:, d % 2, 0:2, :], scaled[:, d % 2, 2:4, :], ALU.add
                                   ).then_inc(partial_made, 1)
                wait_count(pool, chained, 4 * GROUPS * (n - 2) + GROUP)
                pool.wait_ge(partial_made, n + 1)
                pool.tensor_tensor(scaled_sum[:, d % 2, :], partial[:, 0, :], partial[:, 1, :], ALU.add
                                   ).then_inc(scaled_summed, 1)

            def step(i, r, inner):
                tile_ahead = (r + 11) // PER_TILE
                parity, group = tile_ahead % 2, (r + 3) % PER_TILE
                fetch = inner or tile_ahead < TILES
                if inner:
                    t = (i - r) // PER_TILE + tile_ahead
                else:
                    t = tile_ahead
                if fetch and group == 0:
                    wait_count(pool, staged_lo, PER_TILE * (t - 1))
                    wait_count(pool, x_rows_ready, PER_TILE * (t - 1))
                    wait_count(pool, gathered[parity], 16 * F * (t // 2) if isinstance(t, int)
                               else 8 * F * (t - parity))
                    pool.wait_ge(ids_in, 16)
                    take_ids(t, parity)
                for q in range(QUARTERS):
                    if q % GROUPS == 0 and q and has(i, inner, 0):
                        sum_scaled(i, q // GROUPS - 1)
                    if q == 0:
                        if has(i, inner, -1):
                            sum_scaled(i - 1, DQ - 1)
                        pair_low(i, inner, 1, 1)
                    if q == 14:
                        pair_low(i, inner, 0, 2)
                    if q == 12 and has(i, inner, 1):
                        pool.wait_ge(cur_hi_ready, i + 2)
                        wait_count(pool, u_chained_made, 4 * GROUPS * i)
                        pool.tensor_tensor(cur_l[:, 1 - r % 2].rearrange("p d b -> p (d b)"), cur[:, 1 - r % 2],
                                           cur_h[:, 1 - r % 2].rearrange("p d b -> p (d b)").bitcast(F32), ALU.subtract
                                           ).then_inc(cur_lo_ready, 1)
                    if q == 13 and has(i, inner, 1):
                        if (r + 1) % PER_TILE == 0:
                            tiles = (i - r) // PER_TILE + (r + 1) // PER_TILE if inner else (i + 1) // PER_TILE
                            pool.wait_ge(cleared1, tiles + 1)
                        wait_count(pool, cur_summed, i + 1)
                        pool.wait_ge(cur_ready, i + 2)
                        run = run1[:].rearrange("p d b -> p (d b)")
                        pool.tensor_tensor(run, run, cur[:, 1 - r % 2], ALU.add).then_inc(cur_summed, 1)
                    for n in range(4):
                        if GATHER_AT[n] == q and fetch:
                            gather(4 * group + n, parity)

            run_steps(pool, step, 16, 16, 48)

        @block.scalar
        def _(act):
            act.wait_ge(sel_in, 16)
            act.activation(sel[:], sel_raw, ACT.Copy).then_inc(sel_ready, 1)
            act.wait_ge(ident_in, 16)
            act.activation(ident[:], ident_raw, ACT.Copy).then_inc(sel_ready, 1)
            act.wait_ge(w1_summed, 1)
            act.activation(w1_h[:], w1a_raw[:, 0:4, :], ACT.Copy).then_inc(w1_hi, 1)
            act.activation(w1_e[:], w1a_raw[:, 4, :], ACT.Copy).then_inc(w1_hi, 1)
            act.wait_ge(w2_in, 16)
            for n in range(2):
                act.activation(w2_h[:, 16 * n:16 * n + 16, :], w2_raw[:, 16 * n:16 * n + 16, :], ACT.Copy).then_inc(w2_hi, 1)

            def pair_high(i, inner, g, ahead=1):
                if has(i, inner, ahead):
                    if g < 2:
                        act.wait_ge(paired, 5 * (i + ahead) + 2 * g + 2)
                        act.activation(pair_hi[:, 2 * g:2 * g + 2, :], pair_z[:, 2 * g:2 * g + 2, :],
                                       ACT.Copy).then_inc(pair_hi_ready, 1)
                    else:
                        act.wait_ge(paired, 5 * (i + 1) + 5)
                        act.activation(last_hl[:], pair_z[:, 0, :], ACT.Copy).then_inc(pair_hi_ready, 1)

            def scale_group(i, r, inner, q):
                if not has(i, inner, 0):
                    return
                d, g = q // GROUPS, q % GROUPS
                n = DQ * i + d
                if q == 0:
                    if isinstance(i, int) and i == 0:
                        act.wait_ge(w2_lo, 2)
                        act.wait_ge(w1_ready, 3)
                    act.wait_ge(x_rows_ready, i + 1)
                if g == 0:
                    wait_count(act, partial_made, n - 1)
                act.wait_ge(u_scaled_made, GROUPS * n + g + 1)
                for j in range(GROUP):
                    f = GROUP * g + j
                    mul = act.activation(scaled[:, d % 2, g, N * j:N * j + N], bank[:, U_SCALED + g % 2, N * j:N * j + N],
                                         ACT.Copy, scale=x_rows[:, r % 8, f, d:d + 1])
                mul.then_inc(group_scaled, 1)

            def step(i, r, inner):
                k3, tile3 = r + 3, (r + 3) // PER_TILE
                d0 = DQ * (k3 % PER_TILE)
                for q in range(QUARTERS):
                    scale_group(i, r, inner, q)
                    if q == 2 and has(i, inner, 2):
                        act.wait_ge(base_made, i + 3)
                        wait_count(act, paired, 5 * (i + 2))
                        act.activation(base[:], bank[:, TURN, :], ACT.Copy).then_inc(base_ready, 1)
                    if q == 3:
                        pair_high(i, inner, 2, 1)
                    if q == 5 and has(i, inner, 3):
                        act.wait_ge(gathered[tile3 % 2], (i - r) * F + 16 * F * (tile3 // 2 + 1) if inner
                                    else 16 * F * (tile3 // 2 + 1))
                        if inner or i + 3 >= 1:
                            act.wait_ge(turned, i + 3)
                        else:
                            act.wait_ge(zeros_set, 1)
                        act.activation(split_rows[:, :, 0:F],
                                       rows[:, tile3 % 2, :, d0:d0 + DQ].rearrange("p f d -> p d f"),
                                       ACT.Copy).then_inc(staged_hi, 1)
                    if q == 6 and has(i, inner, 3):
                        wait_count(act, chained, 4 * GROUPS * DQ * (i - 4))
                        act.activation(x_rows[:, k3 % 8, :, :], rows[:, tile3 % 2, :, d0:d0 + DQ],
                                       ACT.Copy).then_inc(x_rows_ready, 1)
                    if q == 9 and has(i, inner, 1):
                        act.wait_ge(pair_used, 3 * (i + 1) + 3)
                        wait_count(act, cur_summed, i)
                        wait_count(act, u_chained_made, 4 * GROUPS * i)
                        wait_count(act, cur_lo_ready, i)
                        act.activation(cur[:, 1 - r % 2, :], bank[:, ACC1, :], ACT.Relu).then_inc(cur_ready, 1)
                    if q == 10 and has(i, inner, 1):
                        act.activation(cur_h[:, 1 - r % 2].rearrange("p d b -> p (d b)"), bank[:, ACC1, :],
                                       ACT.Relu).then_inc(cur_hi_ready, 1)
                    if q == 11:
                        pair_high(i, inner, 0, 2)
                    if q == 13 and has(i, inner, 3):
                        act.wait_ge(turned, i + 4)
                        wait_count(act, rotated, 5 * (i + 3))
                        act.activation(x_pair[:], bank[:, TURN, :], ACT.Copy).then_inc(x_pair_ready, 1)
                    if q == 15:
                        pair_high(i, inner, 1, 2)

            run_steps(act, step, 16, 16, 48)

            act.wait_ge(rows_turned, 1)
            act.activation(feat2[:, 0:COLS], bank[:, ROT, :], ACT.Copy).then_inc(feat2_ready, 1)
            act.wait_ge(rows_turned, 2)
            act.activation(feat2[:, COLS:B], bank[:, ROT + 1, :], ACT.Copy).then_inc(feat2_ready, 1)
            act.wait_ge(bias_in, 48)
            for n in range(4):
                act.wait_ge(top_made, n + 1)
                act.activation(h1[:, n, 0:COLS], bank[:, n, :], ACT.Relu, bias=b1_sb[:, n:n + 1]).then_inc(top_act, 1)
            for n in range(2):
                act.wait_ge(top_made, 8 + n + 1)
                act.activation(h2[:, n, 0:COLS], bank[:, n, :], ACT.Relu, bias=b2_sb[:, n:n + 1]).then_inc(top_act, 1)
            act.wait_ge(top_made, 13)
            act.activation(y_row[:, 0:COLS], bank[0:1, 4, :], ACT.Copy).then_inc(top_act, 1)

        @block.vector
        def _(dve):
            dve.memset(split_rows[:].bitcast(F32), 0.0).then_inc(zeros_set, 1)
            dve.memset(run1[:], 0.0).then_inc(cleared1, 1)
            dve.wait_ge(w1_in, 32)
            dve.tensor_tensor(w1a_raw, w1a_raw, w1b_raw, ALU.add).then_inc(w1_summed, 1)
            dve.wait_ge(w1_hi, 2)
            dve.wait_ge(w1_summed, 1)
            dve.tensor_tensor(w1_l[:], w1a_raw[:, 0:4, :], w1_h[:].bitcast(F32), ALU.subtract).then_inc(w1_ready, 1)
            dve.tensor_tensor(w1_e[0:32, :], w1a_raw[0:32, 4, :], w1_e[0:32, :].bitcast(F32),
                              ALU.subtract).then_inc(w1_ready, 1)
            dve.wait_ge(w1_ready, 2)
            dve.tensor_copy(w1_e[0:16, :], w1a_raw[0:16, 4, :]).then_inc(w1_ready, 1)
            for n in range(2):
                dve.wait_ge(w2_hi, n + 1)
                dve.tensor_tensor(w2_l[:, 16 * n:16 * n + 16, :], w2_raw[:, 16 * n:16 * n + 16, :],
                                  w2_h[:, 16 * n:16 * n + 16, :].bitcast(F32), ALU.subtract).then_inc(w2_lo, 1)

            def pair_mul(i, inner, ahead, tiles, r):
                if not has(i, inner, ahead):
                    return
                for a in tiles:
                    n = 5 * (i + ahead) + a
                    dve.wait_ge(rotated, n + 1)
                    if a == 0:
                        dve.wait_ge(base_ready, i + ahead + 1)
                    g = a // 2
                    wait_count(dve, pair_used, 3 * (i + ahead - 1) + g + 1)
                    if a == 4:
                        dve.wait_ge(pair_lo_ready[0], i + ahead + 1)
                    if a == 0:
                        wait_count(dve, pair_lo_ready[2], i + ahead)
                    dve.tensor_tensor(pair_z[:, a % 4, :], bank[:, ROT + (r + ahead + a) % 2, :], base[:], ALU.mult).then_inc(paired, 1)

            def pair_low(i, inner, g, ahead=1):
                if g < 2 and PAIR_SPLIT[g] != "D" or not has(i, inner, ahead):
                    return
                dve.wait_ge(pair_hi_ready, 3 * (i + ahead) + g + 1)
                if g < 2:
                    dve.tensor_tensor(pair_lo[:, 2 * g:2 * g + 2, :], pair_z[:, 2 * g:2 * g + 2, :],
                                      pair_hi[:, 2 * g:2 * g + 2, :].bitcast(F32), ALU.subtract
                                      ).then_inc(pair_lo_ready[g], 1)
                else:
                    dve.tensor_tensor(last_hl[32:64, :], pair_z[32:64, 0, :], last_hl[32:64, :].bitcast(F32),
                                      ALU.subtract).then_inc(pair_lo_ready[2], 1)

            def chain_group(i, r, inner, d, g):
                block_of, slot = (i, r) if d < 2 else (i - 1, r - 1)
                n = DQ * block_of + d
                m = 4 * GROUPS * n + GROUP * g
                if g == 0:
                    dve.wait_ge(scaled_summed, n + 1)
                    if d % 2 == 0:
                        wait_count(dve, chains_halved, 2 * block_of - 1 + d // 2)
                    if isinstance(n, int) and n == 0:
                        dve.wait_ge(w2_lo, 2)
                        dve.wait_ge(x_rows_ready, 1)
                dve.wait_ge(u_chained_made, GROUPS * n + g + 1)
                for j in range(GROUP):
                    if g:
                        dve.wait_ge(chained, m + j - 3)
                    before = chain[:, d, j, :] if g else scaled_sum[:, d % 2, N * j:N * j + N]
                    dve.scalar_tensor_tensor(chain[:, d, j, :], bank[:, U_CHAINED + g % 2, N * j:N * j + N],
                                             x_rows[:, slot % 8, GROUP * (GROUPS + g) + j, d:d + 1], before,
                                             ALU.mult, ALU.add).then_inc(chained, 1)

            def halve_chains(i, inner, columns):
                if has(i, inner, -1):
                    first = 2 * columns
                    dve.wait_ge(chained, 4 * GROUPS * (DQ * (i - 1) + first + 2))
                    wait_count(dve, out2_made, i - 1)
                    dve.tensor_tensor(halves[:, first:first + 2], chain[:, first:first + 2, 0:2, :],
                                      chain[:, first:first + 2, 2:4, :], ALU.add).then_inc(chains_halved, 1)

            def join_chains(i, inner):
                if has(i, inner, -1):
                    dve.wait_ge(chains_halved, 2 * i)
                    wait_count(dve, out2_summed, i - 1)
                    dve.tensor_tensor(out2[:], halves[:, :, 0, :], halves[:, :, 1, :], ALU.add).then_inc(out2_made, 1)

            def sum_layer2(i, r, inner):
                if not has(i, inner, -1):
                    return
                flat_run = run2[:].rearrange("p d b -> p (d b)")
                source = out2[:].rearrange("p d b -> p (d b)")
                dve.wait_ge(out2_made, i)
                if (r - 1) % PER_TILE == 0:
                    wait_count(dve, folded2, tiles_before(i, r, inner, -1))
                    dve.tensor_scalar(flat_run, source, 0.0, None, ALU.max).then_inc(out2_summed, 1)
                else:
                    dve.wait_ge(out2_summed, i - 1)
                    dve.scalar_tensor_tensor(flat_run, source, 0.0, flat_run, ALU.max, ALU.add
                                             ).then_inc(out2_summed, 1)
                if (r - 1) % PER_TILE == PER_TILE - 1:
                    dve.wait_ge(out2_summed, i)
                    t = tiles_before(i, r, inner, -1)
                    rows_of = feat2_rows[:, t, :] if isinstance(t, int) else feat2_rows[:, bass.ds(t, 1), :].rearrange("p a n -> p (a n)")
                    fold(t, rows_of, run2, halved2, folded2)

            def fold_layer1(i, r, inner):
                if has(i, inner, 1) and (r + 1) % PER_TILE == PER_TILE - 1:
                    dve.wait_ge(cur_summed, i + 2)
                    t = tiles_before(i, r, inner, 1)
                    cols = bass.ds((i - r) * (P // PER_TILE) + P * ((r + 1) // PER_TILE), P) if inner \
                        else slice(P * t, P * t + P)
                    fold(t, feat1[:, cols], run1, halved1, folded1)
                    dve.wait_ge(folded1, tiles_before(i, r, inner, 1) + 1)
                    dve.memset(run1[:], 0.0).then_inc(cleared1, 1)

            def tiles_before(i, r, inner, ahead):
                return (i - r) // PER_TILE + (r + ahead) // PER_TILE if inner else (i + ahead) // PER_TILE

            def fold(t, features, run, halved, folded):
                dve.tensor_tensor(run[:, 0:2, :], run[:, 0:2, :], run[:, 2:4, :], ALU.add).then_inc(halved, 1)
                dve.wait_ge(halved, t + 1)
                dve.tensor_tensor(features, run[:, 0, :], run[:, 1, :], ALU.add).then_inc(folded, 1)

            def step(i, r, inner):
                for q in range(QUARTERS):
                    if has(i, inner, 0 if q >= 2 * GROUPS else -1):
                        chain_group(i, r, inner, (q // GROUPS + 2) % DQ, q % GROUPS)
                    if q == 1:
                        pair_mul(i, inner, 1, (4,), r)
                    if q == 3:
                        halve_chains(i, inner, 0)
                    if q == 5:
                        pair_low(i, inner, 2, 1)
                    if q == 6:
                        pair_mul(i, inner, 2, (0,), r)
                    if q == 7:
                        pair_mul(i, inner, 2, (1,), r)
                    if q == 8:
                        halve_chains(i, inner, 1)
                    if q == 9 and has(i, inner, 3):
                        dve.wait_ge(staged_hi, i + 4)
                        k3 = r + 3
                        d0 = DQ * (k3 % PER_TILE)
                        dve.tensor_tensor(split_rows[:, :, F:2 * F],
                                          rows[:, (k3 // PER_TILE) % 2, :, d0:d0 + DQ].rearrange("p f d -> p d f"),
                                          split_rows[:, :, 0:F].bitcast(F32), ALU.subtract).then_inc(staged_lo, 1)
                    if q == 10:
                        join_chains(i, inner)
                    if q == 11:
                        pair_mul(i, inner, 2, (2,), r)
                    if q == 12:
                        pair_mul(i, inner, 2, (3,), r)
                    if q == 13:
                        sum_layer2(i, r, inner)
                    if q == 14:
                        pair_low(i, inner, 0, 2)
                    if q == 15:
                        fold_layer1(i, r, inner)

            run_steps(dve, step, 16, 16, 48)

            dve.wait_ge(bias_in, 48)
            for n in range(4):
                dve.wait_ge(top_made, 4 + n + 1)
                dve.tensor_scalar(h1[:, n, COLS:B], bank[:, 4 + n, :], b1_sb[:, n:n + 1], 0.0,
                                  ALU.add, ALU.max).then_inc(top_dve, 1)
            for n in range(2):
                dve.wait_ge(top_made, 10 + n + 1)
                dve.tensor_scalar(h2[:, n, COLS:B], bank[:, 2 + n, :], b2_sb[:, n:n + 1], 0.0,
                                  ALU.add, ALU.max).then_inc(top_dve, 1)
            dve.wait_ge(top_made, 14)
            dve.tensor_copy(y_row[:, COLS:B], bank[0:1, 5, :]).then_inc(top_dve, 1)

        @block.tensor
        def _(pe):
            pe.wait_ge(sel_ready, 2)

            def rotate(i, inner, ahead, tiles, parity):
                if has(i, inner, ahead):
                    for a in tiles:
                        wait_count(pe, paired, 5 * (i + ahead) + a - 1)
                        pe.matmul(bank[:, ROT + (parity + ahead + a) % 2, :], sel[:, SEL_ROT + a, :], x_pair[:],
                                  start=True, stop=True).then_inc(rotated, 1)

            def split_product(acc, wh, wl, hi, lo, start, stop):
                pe.matmul(acc, wh, hi, start=start, stop=False)
                pe.matmul(acc, wl, hi, start=False, stop=False)
                return pe.matmul(acc, wh, lo, start=False, stop=stop)

            def pair_products(i, inner, ahead, a):
                g = a // 2
                if not has(i, inner, ahead):
                    return
                k = i + ahead
                acc = bank[:, ACC1, :]
                if a == 0:
                    wait_count(pe, cur_hi_ready, k)
                    if isinstance(k, int) and k == 0:
                        pe.wait_ge(w1_ready, 3)
                pe.wait_ge(pair_hi_ready, 3 * k + g + 1)
                pe.wait_ge(pair_lo_ready[g], k + 1)
                if g < 2:
                    mm = split_product(acc, w1_h[:, a, :], w1_l[:, a, :], pair_hi[:, a, :], pair_lo[:, a, :], a == 0, False)
                else:
                    mm = pe.matmul(acc, w1_e[:], last_hl[:], start=False, stop=True)
                if a % 2 or g == 2:
                    mm.then_inc(pair_used, 1)

            def group_products(acc, fields, d, parity):
                return split_product(acc, cur_h[:, parity, d, :], cur_l[:, parity, d, :],
                                     w2_h[:, fields:fields + GROUP, :], w2_l[:, fields:fields + GROUP, :], True, True)

            def scaled_group(i, inner, d, g, parity):
                if has(i, inner, 0):
                    n = GROUPS * (DQ * i + d) + g
                    if d == 0 and g == 0:
                        pe.wait_ge(cur_lo_ready, i + 1)
                        if isinstance(i, int) and i == 0:
                            pe.wait_ge(w2_lo, 2)
                    wait_count(pe, group_scaled, n - 1)
                    group_products(bank[:, U_SCALED + g % 2, :], GROUP * g, d, parity).then_inc(u_scaled_made, 1)

            def chained_group(i, inner, d, g, parity):
                ahead = 0 if d < 2 else -1
                if has(i, inner, ahead):
                    n = GROUPS * (DQ * (i + ahead) + d) + g
                    wait_count(pe, chained, GROUP * (n - 1))
                    group_products(bank[:, U_CHAINED + g % 2, :], GROUP * (GROUPS + g), d,
                                   (parity + ahead) % 2).then_inc(u_chained_made, 1)

            def step(i, r, inner):
                parity = r % 2
                for q in range(QUARTERS):
                    scaled_group(i, inner, q // GROUPS, q % GROUPS, parity)
                    chained_group(i, inner, (q // GROUPS + 2) % DQ, q % GROUPS, parity)
                    if q in (0, 1):
                        pair_products(i, inner, 1, q)
                    if q in (2, 3):
                        rotate(i, inner, 2, (q - 2,), parity)
                    if q in (4, 5):
                        pair_products(i, inner, 1, q - 2)
                    if q == 7:
                        pair_products(i, inner, 1, 4)
                    if q in (8, 9):
                        rotate(i, inner, 2, (q - 6,), parity)
                    if q == 11 and has(i, inner, 3):
                        pe.wait_ge(staged_lo, i + 4)
                        wait_count(pe, base_ready, i + 3)
                        for d in range(DQ):
                            mm = pe.matmul(bank[:, TURN, P * d:P * d + P], split_rows[:, d, :], ident[:],
                                           start=True, stop=True)
                        mm.then_inc(turned, 1)
                    if q == 13:
                        rotate(i, inner, 2, (4,), parity)
                    if q == 15 and has(i, inner, 3):
                        pe.wait_ge(x_pair_ready, i + 4)
                        pe.matmul(bank[:, TURN, :], sel[:, SEL_BASE, :], x_pair[:], start=True, stop=True
                                  ).then_inc(base_made, 1)

            run_steps(pe, step, 2, 2, BLOCKS - 4)

            for half in range(2):
                pe.wait_ge(folded2, 4 * half + 4)
                for t in range(4):
                    mm = pe.matmul(bank[:, ROT + half, P * t:P * t + P], feat2_rows[:, 4 * half + t, :], ident[:].bitcast(F32),
                                   start=True, stop=True)
                mm.then_inc(rows_turned, 1)
            pe.wait_ge(top_in, 64)
            pe.wait_ge(bias_in, 48)
            pe.wait_ge(folded1, TILES)
            pe.wait_ge(feat2_ready, 2)
            for half in range(2):
                cols = slice(COLS * half, COLS * half + COLS)
                for n in range(4):
                    acc, m = bank[:, 4 * half + n, :], slice(P * n, P * n + P)
                    pe.matmul(acc, wt1_sb[:, 0, m], feat1[:, cols], start=True, stop=False)
                    pe.matmul(acc, wt1_sb[:, 1, m], feat2[:, cols], start=False, stop=False)
                    pe.matmul(acc, wt1d_sb[:, m], dense_sb[:, cols], start=False, stop=True).then_inc(top_made, 1)
            for half, done in ((0, top_act), (1, top_dve)):
                pe.wait_ge(done, 4)
                if half:
                    pe.wait_ge(top_act, 4)
                cols = slice(COLS * half, COLS * half + COLS)
                for n in range(2):
                    acc = bank[:, 2 * half + n, :]
                    for c in range(4):
                        mm = pe.matmul(acc, wt2_sb[:, c, P * n:P * n + P], h1[:, c, cols], start=(c == 0), stop=(c == 3))
                    mm.then_inc(top_made, 1)
            for half, done in ((0, top_act), (1, top_dve)):
                pe.wait_ge(done, 6)
                for c in range(2):
                    mm = pe.matmul(bank[0:1, 4 + half, :], wt3_sb[:, c:c + 1], h2[:, c, COLS * half:COLS * half + COLS],
                                   start=(c == 0), stop=(c == 1))
                mm.then_inc(top_made, 1)


def layouts():
    import numpy as np
    r = np.arange(P)
    kk, m = r // 32, r % 32
    first = np.zeros((P, 5), np.int64)
    second = np.zeros((P, 5), np.int64)
    for a in range(4):
        other = (m + 4 * a + kk) % F
        first[:, a], second[:, a] = m * F + other, other * F + m
    m16 = r % 16
    first[:, 4], second[:, 4] = m16 * F + m16 + 16, (m16 + 16) * F + m16
    sel = np.zeros((P, N_SEL, P), np.float32)
    for half in (0, 32):
        sel[half + m, SEL_BASE, r] = 1.0
        for a in range(4):
            sel[half + (m + 4 * a + kk) % F, SEL_ROT + a, r] = 1.0
        sel[half + (m + 16) % F, SEL_ROT + 4, r] = 1.0
    return first, second, sel, np.eye(P, dtype=np.float32)


def kernel(**inputs):
    import numpy as np
    import concourse.bacc as bacc
    from concourse.bass_utils import run_bass_kernel_spmd

    first, second, sel, eye = layouts()
    f0 = np.asarray(inputs["L0_rec_filter_0"])[0]
    f1 = np.asarray(inputs["L0_rec_filter_1"])[0]
    w1a = f0[first]
    w1b = f0[second]
    w1b[:F, 0] = 0
    w1a[48:, 4] = 0
    w1b[48:, 4] = 0
    w2 = f1.reshape(F, N, N).transpose(1, 0, 2)
    wt1 = np.asarray(inputs["W_top1"])
    arrays = {
        "ids": np.asarray(inputs["ids"]).reshape(TILES, P, F).transpose(1, 0, 2),
        **{f"tbl_{f}": np.asarray(inputs[f"tbl_{f}"]) for f in range(F)},
        "w1a": w1a, "w1b": w1b, "w2": w2, "selectors": sel, "identity": eye,
        "dense": np.asarray(inputs["dense_ctx"]).T,
        "wt1": wt1[:2 * N].reshape(2, P, H1).transpose(1, 0, 2),
        "wt1d": wt1[2 * N:],
        "b1": np.asarray(inputs["b_top1"]).reshape(H1 // P, P).T,
        "wt2": np.asarray(inputs["W_top2"]).reshape(4, P, H2).transpose(1, 0, 2),
        "b2": np.asarray(inputs["b_top2"]).reshape(H2 // P, P).T,
        "wt3": np.asarray(inputs["W_top3"]).reshape(H2 // P, P).T,
    }
    arrays = {name: np.ascontiguousarray(a) for name, a in arrays.items()}
    nc = bacc.Bacc("TRN2", target_bir_lowering=False, num_devices=1)
    ap = {name: nc.dram_tensor(name, a.shape, mybir.dt.from_np(a.dtype), kind="ExternalInput").ap()
          for name, a in arrays.items()}
    y = nc.dram_tensor("y", (1, B), F32, kind="ExternalOutput").ap()
    build_program(nc, ap["ids"], [ap[f"tbl_{f}"] for f in range(F)], ap["w1a"], ap["w1b"], ap["w2"], ap["selectors"],
                  ap["identity"], ap["dense"], ap["wt1"], ap["wt1d"], ap["b1"], ap["wt2"], ap["b2"], ap["wt3"], y)
    r = run_bass_kernel_spmd(nc, [arrays], core_ids=[0])
    return r.results[0]["y"].reshape(B, 1)
```

```python
from contextlib import ExitStack

import concourse.bass as bass
from concourse import mybir

F32 = mybir.dt.float32
F32R = mybir.dt.float32r
I32 = mybir.dt.int32
ALU = mybir.AluOpType
ACT = mybir.ActivationFunctionType

P = 128
B = 1024
F = 32
D = 32
N = 128
DQ = 4
COLS = DQ * P
TILES = B // P
PER_TILE = D // DQ
BLOCKS = TILES * PER_TILE
GROUP = 4
GROUPS = F // GROUP // 2
QUARTERS = GROUPS * DQ
DENSE = 16
H1, H2 = 512, 256

PE_AT = {"turn_3": 11, "base_3": 15, "rotate_2": (3, 4, 8, 10, 13), "pairs_1": (1, 3, 5, 7, 7)}
ACT_AT = {"rows_high_3": 5, "rows_3": 6, "x_pair_3": 13, "base_2": 2, "pair_high_2": (11, 15), "last_high_1": 4,
          "cur_1": 8, "cur_high_1": 10}
DVE_AT = {"rows_low_3": 9, "multiply_2": (6, 7, 11, 12), "pair_low_2": 15, "multiply_1": 1, "last_low_1": 5,
          "halve": (3, 8), "join": 10, "sum": 13, "fold": 15}
POOL_AT = {"sum": 0, "pair_low_1": 0, "cur_low_1": 12, "cur_sum_1": 15, "gather": (2, 6, 10, 13)}
SEL_BASE, SEL_ROT = 0, 1
N_SEL = 6


def wait_count(engine, semaphore, count):
    if not (isinstance(count, int) and count <= 0):
        engine.wait_ge(semaphore, count)


def build_program(nc, ids, tables, w1a, w1b, w2, selectors, identity, dense, wt1, wt1d, b1, wt2, b2, wt3, out):
    with ExitStack() as ctx:
        def sb(name, shape, dt=F32):
            return ctx.enter_context(nc.sbuf_tensor(name, shape, dt))

        def sem(name):
            return ctx.enter_context(nc.semaphore(name))

        ids_all = sb("ids_all", [P, TILES, F], I32)
        ids_now = sb("ids_now", [P, 2, F], I32)
        rows = sb("rows", [P, 2, F, D])
        split_rows = sb("split_rows", [P, DQ, P], F32R)
        x_pair = sb("x_pair", [P, COLS], F32R)
        x_rows = sb("x_rows", [P, 8, F, DQ])
        base = sb("base", [P, COLS])
        pair_z = sb("pair_z", [P, 4, COLS])
        pair_hi = sb("pair_hi", [P, 4, COLS], F32R)
        pair_lo = sb("pair_lo", [P, 4, COLS], F32R)
        last_hl = sb("last_hl", [P, COLS], F32R)
        cur = sb("cur", [P, 2, COLS])
        cur_h = sb("cur_h", [P, 2, DQ, P], F32R)
        cur_l = sb("cur_l", [P, 2, DQ, P], F32R)
        work = sb("work", [P, 7 * B])
        scaled_sum = sb("scaled_sum", [P, 2, COLS])
        halves = sb("halves", [P, DQ, 2, N])
        out2 = sb("out2", [P, DQ, N])
        run1 = sb("run1", [P, DQ, P])
        run2 = sb("run2", [P, DQ, P])
        feat2_rows = sb("feat2_rows", [P, TILES, N])
        feat1 = sb("feat1", [P, B])
        feat2 = sb("feat2", [P, B])
        w1_h = sb("w1_h", [P, 4, N], F32R)
        w1_l = sb("w1_l", [P, 4, N], F32R)
        w1_e = sb("w1_e", [P, N], F32R)
        w2_h = sb("w2_h", [P, F, N], F32R)
        w2_l = sb("w2_l", [P, F, N], F32R)
        sel = sb("sel", [P, N_SEL, P], F32R)
        ident = sb("ident", [P, P], F32R)
        b1_sb = sb("b1_sb", [P, H1 // P])
        b2_sb = sb("b2_sb", [P, H2 // P])
        wt3_sb = sb("wt3_sb", [P, H2 // P])
        wt1_sb = sb("wt1_sb", [P, 2, H1])
        wt1d_sb = sb("wt1d_sb", [DENSE, H1])
        dense_sb = sb("dense_sb", [DENSE, B])
        wt2_sb = sb("wt2_sb", [P, 4, H2])
        ns, n1 = N_SEL * P, 5 * N
        w2_raw = work[:, 0:F * N].rearrange("p (c n) -> p c n", n=N)
        at = F * N
        sel_raw = work[:, at:at + ns].rearrange("p (c n) -> p c n", n=P)
        w1a_raw = work[:, at + ns:at + ns + n1].rearrange("p (c n) -> p c n", n=N)
        w1b_raw = work[:, at + ns + n1:at + ns + 2 * n1].rearrange("p (c n) -> p c n", n=N)
        ident_raw = work[:, at + ns + 2 * n1:at + ns + 2 * n1 + P]
        scaled = work[:, 0:4 * B].rearrange("p (a g n) -> p a g n", a=2, g=GROUPS)
        chain = work[:, 4 * B:6 * B].rearrange("p (d j n) -> p d j n", d=DQ, j=GROUP)
        partial = work[:, 6 * B:7 * B].rearrange("p (a n) -> p a n", a=2)
        h1 = work[:, 0:4 * B].rearrange("p (c b) -> p c b", c=4)
        h2 = work[:, 4 * B:6 * B].rearrange("p (c b) -> p c b", c=2)
        y_row = work[0:1, 6 * B:7 * B]

        bank = ctx.enter_context(nc.psum_tensor("bank", [P, 8, COLS], F32))
        U_SCALED, U_CHAINED, ACC1, TURN, ROT = 0, 2, 4, 5, 6
        TOP = ((0, 1, 4, 5), (2, 3, 6, 7))

        ids_in = sem("ids_in")
        w1_in, w2_in, sel_in, ident_in = sem("w1_in"), sem("w2_in"), sem("sel_in"), sem("ident_in")
        zeros_set = sem("zeros_set")
        sel_ready, w1_summed, w1_hi, w1_ready = sem("sel_ready"), sem("w1_summed"), sem("w1_hi"), sem("w1_ready")
        w2_hi, w2_lo = sem("w2_hi"), sem("w2_lo")
        ids_copied = sem("ids_copied")
        gathered = [sem("gathered_even"), sem("gathered_odd")]
        staged_hi, staged_lo = sem("staged_hi"), sem("staged_lo")
        turned, x_pair_ready, x_rows_ready = sem("turned"), sem("x_pair_ready"), sem("x_rows_ready")
        base_made, base_ready = sem("base_made"), sem("base_ready")
        rotated, paired = sem("rotated"), sem("paired")
        pair_hi_ready = sem("pair_hi_ready")
        pair_lo_ready = [sem("pair_lo0_ready"), sem("pair_lo1_ready"), sem("pair_lo2_ready")]
        pair_used = sem("pair_used")
        cur_ready, cur_summed = sem("cur_ready"), sem("cur_summed")
        cur_hi_ready, cur_lo_ready = sem("cur_hi_ready"), sem("cur_lo_ready")
        u_scaled_made, u_chained_made = sem("u_scaled_made"), sem("u_chained_made")
        group_scaled, partial_made, scaled_summed = sem("group_scaled"), sem("partial_made"), sem("scaled_summed")
        chained, chains_halved = sem("chained"), sem("chains_halved")
        out2_made, out2_summed = sem("out2_made"), sem("out2_summed")
        rows_turned, feat2_ready = sem("rows_turned"), sem("feat2_ready")
        folded1, folded2 = sem("folded1"), sem("folded2")
        halved1, halved2, cleared1 = sem("halved1"), sem("halved2"), sem("cleared1")
        top_in, bias_in = sem("top_in"), sem("bias_in")
        top_made, top_act, top_dve, y_out = sem("top_made"), sem("top_act"), sem("top_dve"), sem("y_out")

        block = ctx.enter_context(nc.Block())

        def has(i, inner, ahead):
            return inner or 0 <= i + ahead < BLOCKS

        def run_steps(engine, step, unroll, first, last):
            for i in range(-3, first):
                step(i, i, False)
            with engine.Fori(first // unroll, last // unroll) as q:
                for r in range(unroll):
                    step(q * unroll + r, r, True)
            for i in range(last, BLOCKS + 1):
                step(i, i, False)

        @block.sync
        def _(sp):
            sp.dma_start(ids_all[:], ids).then_inc(ids_in, 16)
            sp.dma_start(sel_raw, selectors).then_inc(sel_in, 16)
            sp.dma_start(ident_raw, identity).then_inc(ident_in, 16)
            sp.dma_start(w1a_raw, w1a).then_inc(w1_in, 16)
            sp.dma_start(w1b_raw, w1b).then_inc(w1_in, 16)
            sp.dma_start(w2_raw, w2).then_inc(w2_in, 16)
            sp.dma_start(b1_sb[:], b1).then_inc(bias_in, 16)
            sp.dma_start(b2_sb[:], b2).then_inc(bias_in, 16)
            sp.dma_start(wt3_sb[:], wt3).then_inc(bias_in, 16)
            sp.dma_start(wt1_sb[:], wt1).then_inc(top_in, 16)
            sp.dma_start(wt1d_sb[:], wt1d).then_inc(top_in, 16)
            sp.dma_start(dense_sb[:], dense).then_inc(top_in, 16)
            sp.dma_start(wt2_sb[:], wt2).then_inc(top_in, 16)
            sp.wait_ge(top_act, 7)
            sp.wait_ge(top_dve, 7)
            sp.dma_start(out, y_row).then_inc(y_out, 16)
            sp.wait_ge(y_out, 16)

        @block.gpsimd
        def _(pool):
            pool.wait_ge(ids_in, 16)

            def take_ids(t, parity):
                pool.tensor_copy(ids_now[:, parity, :], ids_all[:, t, :] if isinstance(t, int)
                                 else ids_all[:, bass.ds(t, 1), :]).then_inc(ids_copied, 1)
                pool.wait_ge(ids_copied, t + 1)

            def gather(f, parity):
                pool.indirect_dma_start(rows[:, parity, f, :], None, tables[f],
                                        bass.IndirectOffsetOnAxis(ids_now[:, parity, f:f + 1], 0)
                                        ).then_inc(gathered[parity], 16)

            take_ids(0, 0)
            for f in range(F):
                gather(f, 0)

            def pair_low(i, inner):
                if has(i, inner, 1):
                    pool.wait_ge(pair_hi_ready, 3 * (i + 1) + 2)
                    pool.tensor_tensor(pair_lo[:, 2:4, :], pair_z[:, 2:4, :], pair_hi[:, 2:4, :].bitcast(F32), ALU.subtract
                                       ).then_inc(pair_lo_ready[1], 1)

            def sum_scaled(k, d):
                n = DQ * k + d
                pool.wait_ge(group_scaled, GROUPS * (n + 1))
                wait_count(pool, scaled_summed, n)
                pool.tensor_tensor(partial, scaled[:, d % 2, 0:2, :], scaled[:, d % 2, 2:4, :], ALU.add
                                   ).then_inc(partial_made, 1)
                wait_count(pool, chained, 4 * GROUPS * (n - 2) + GROUP)
                pool.wait_ge(partial_made, n + 1)
                pool.tensor_tensor(scaled_sum[:, d % 2, :], partial[:, 0, :], partial[:, 1, :], ALU.add
                                   ).then_inc(scaled_summed, 1)

            def step(i, r, inner):
                tile_ahead = (r + 11) // PER_TILE
                parity, group = tile_ahead % 2, (r + 3) % PER_TILE
                fetch = inner or tile_ahead < TILES
                t = (i - r) // PER_TILE + tile_ahead if inner else tile_ahead
                if fetch and group == 0:
                    wait_count(pool, staged_lo, PER_TILE * (t - 1))
                    wait_count(pool, x_rows_ready, PER_TILE * (t - 1))
                    wait_count(pool, gathered[parity], 16 * F * (t // 2) if isinstance(t, int)
                               else 8 * F * (t - parity))
                    pool.wait_ge(ids_in, 16)
                    take_ids(t, parity)
                for q in range(QUARTERS):
                    if q % GROUPS == POOL_AT["sum"]:
                        d = q // GROUPS - 1
                        if has(i, inner, 0 if d >= 0 else -1):
                            sum_scaled(i if d >= 0 else i - 1, d % DQ)
                    if q == POOL_AT["pair_low_1"]:
                        pair_low(i, inner)
                    if q == POOL_AT["cur_low_1"] and has(i, inner, 1):
                        pool.wait_ge(cur_hi_ready, i + 2)
                        wait_count(pool, u_chained_made, 4 * GROUPS * i)
                        pool.tensor_tensor(cur_l[:, 1 - r % 2].rearrange("p d b -> p (d b)"), cur[:, 1 - r % 2],
                                           cur_h[:, 1 - r % 2].rearrange("p d b -> p (d b)").bitcast(F32), ALU.subtract
                                           ).then_inc(cur_lo_ready, 1)
                    if q == POOL_AT["cur_sum_1"] and has(i, inner, 1):
                        if (r + 1) % PER_TILE == 0:
                            tiles = (i - r) // PER_TILE + (r + 1) // PER_TILE if inner else (i + 1) // PER_TILE
                            pool.wait_ge(cleared1, tiles + 1)
                        wait_count(pool, cur_summed, i + 1)
                        pool.wait_ge(cur_ready, i + 2)
                        run = run1[:].rearrange("p d b -> p (d b)")
                        pool.tensor_tensor(run, run, cur[:, 1 - r % 2], ALU.add).then_inc(cur_summed, 1)
                    for n in range(4):
                        if POOL_AT["gather"][n] == q and fetch:
                            gather(4 * group + n, parity)

            run_steps(pool, step, 16, 16, 48)

        @block.scalar
        def _(act):
            act.wait_ge(sel_in, 16)
            act.activation(sel[:], sel_raw, ACT.Copy).then_inc(sel_ready, 1)
            act.wait_ge(ident_in, 16)
            act.activation(ident[:], ident_raw, ACT.Copy).then_inc(sel_ready, 1)
            act.wait_ge(w1_summed, 1)
            act.activation(w1_h[:], w1a_raw[:, 0:4, :], ACT.Copy).then_inc(w1_hi, 1)
            act.activation(w1_e[:], w1a_raw[:, 4, :], ACT.Copy).then_inc(w1_hi, 1)
            act.wait_ge(w2_in, 16)
            for n in range(2):
                act.activation(w2_h[:, 16 * n:16 * n + 16, :], w2_raw[:, 16 * n:16 * n + 16, :], ACT.Copy
                               ).then_inc(w2_hi, 1)

            def pair_high(i, inner, g):
                if has(i, inner, 2):
                    act.wait_ge(paired, 5 * (i + 2) + 2 * g + 2)
                    act.activation(pair_hi[:, 2 * g:2 * g + 2, :], pair_z[:, 2 * g:2 * g + 2, :],
                                   ACT.Copy).then_inc(pair_hi_ready, 1)

            def scale_group(i, r, inner, q):
                if not has(i, inner, 0):
                    return
                d, g = q // GROUPS, q % GROUPS
                n = DQ * i + d
                if q == 0:
                    if isinstance(i, int) and i == 0:
                        act.wait_ge(w2_lo, 2)
                        act.wait_ge(w1_ready, 3)
                    act.wait_ge(x_rows_ready, i + 1)
                if g == 0:
                    wait_count(act, partial_made, n - 1)
                act.wait_ge(u_scaled_made, GROUPS * n + g + 1)
                for j in range(GROUP):
                    f = GROUP * g + j
                    mul = act.activation(scaled[:, d % 2, g, N * j:N * j + N], bank[:, U_SCALED + g % 2, N * j:N * j + N],
                                         ACT.Copy, scale=x_rows[:, r % 8, f, d:d + 1])
                mul.then_inc(group_scaled, 1)

            def step(i, r, inner):
                k3, tile3 = r + 3, (r + 3) // PER_TILE
                d0 = DQ * (k3 % PER_TILE)
                for q in range(QUARTERS):
                    scale_group(i, r, inner, q)
                    if q == ACT_AT["base_2"] and has(i, inner, 2):
                        act.wait_ge(base_made, i + 3)
                        wait_count(act, paired, 5 * (i + 2))
                        act.activation(base[:], bank[:, TURN, :], ACT.Copy).then_inc(base_ready, 1)
                    if q == ACT_AT["last_high_1"] and has(i, inner, 1):
                        act.wait_ge(paired, 5 * (i + 1) + 5)
                        act.activation(last_hl[:], pair_z[:, 0, :], ACT.Copy).then_inc(pair_hi_ready, 1)
                    if q == ACT_AT["rows_high_3"] and has(i, inner, 3):
                        act.wait_ge(gathered[tile3 % 2], (i - r) * F + 16 * F * (tile3 // 2 + 1) if inner
                                    else 16 * F * (tile3 // 2 + 1))
                        if inner or i + 3 >= 1:
                            act.wait_ge(turned, i + 3)
                        else:
                            act.wait_ge(zeros_set, 1)
                        act.activation(split_rows[:, :, 0:F],
                                       rows[:, tile3 % 2, :, d0:d0 + DQ].rearrange("p f d -> p d f"),
                                       ACT.Copy).then_inc(staged_hi, 1)
                    if q == ACT_AT["rows_3"] and has(i, inner, 3):
                        wait_count(act, chained, 4 * GROUPS * DQ * (i - 4))
                        act.activation(x_rows[:, k3 % 8, :, :], rows[:, tile3 % 2, :, d0:d0 + DQ],
                                       ACT.Copy).then_inc(x_rows_ready, 1)
                    if q == ACT_AT["cur_1"] and has(i, inner, 1):
                        act.wait_ge(pair_used, 3 * (i + 1) + 3)
                        wait_count(act, cur_summed, i)
                        wait_count(act, u_chained_made, 4 * GROUPS * i)
                        wait_count(act, cur_lo_ready, i)
                        act.activation(cur[:, 1 - r % 2, :], bank[:, ACC1, :], ACT.Relu).then_inc(cur_ready, 1)
                    if q == ACT_AT["cur_high_1"] and has(i, inner, 1):
                        act.activation(cur_h[:, 1 - r % 2].rearrange("p d b -> p (d b)"), bank[:, ACC1, :],
                                       ACT.Relu).then_inc(cur_hi_ready, 1)
                    if q == ACT_AT["pair_high_2"][0]:
                        pair_high(i, inner, 0)
                    if q == ACT_AT["x_pair_3"] and has(i, inner, 3):
                        act.wait_ge(turned, i + 4)
                        wait_count(act, rotated, 5 * (i + 3))
                        act.activation(x_pair[:], bank[:, TURN, :], ACT.Copy).then_inc(x_pair_ready, 1)
                    if q == ACT_AT["pair_high_2"][1]:
                        pair_high(i, inner, 1)

            run_steps(act, step, 16, 16, 48)

            act.wait_ge(rows_turned, 1)
            act.activation(feat2[:, 0:COLS], bank[:, ROT, :], ACT.Copy).then_inc(feat2_ready, 1)
            act.wait_ge(bias_in, 48)
            act.wait_ge(partial_made, DQ * BLOCKS)
            for n in range(4):
                act.wait_ge(top_made, n + 1)
                act.activation(h1[:, n, 0:COLS], bank[:, TOP[0][n], :], ACT.Relu, bias=b1_sb[:, n:n + 1]
                               ).then_inc(top_act, 1)
            act.wait_ge(chains_halved, 2 * BLOCKS)
            for n in range(2):
                act.wait_ge(top_made, 4 + n + 1)
                act.activation(h2[:, n, 0:COLS], bank[:, n, :], ACT.Relu, bias=b2_sb[:, n:n + 1]).then_inc(top_act, 1)
            act.wait_ge(rows_turned, 2)
            act.activation(feat2[:, COLS:B], bank[:, ROT + 1, :], ACT.Copy).then_inc(feat2_ready, 1)
            act.wait_ge(top_made, 11)
            act.activation(y_row[:, 0:COLS], bank[0:1, 4, :], ACT.Copy).then_inc(top_act, 1)

        @block.vector
        def _(dve):
            dve.memset(split_rows[:].bitcast(F32), 0.0).then_inc(zeros_set, 1)
            dve.memset(run1[:], 0.0).then_inc(cleared1, 1)
            dve.wait_ge(w1_in, 32)
            dve.tensor_tensor(w1a_raw, w1a_raw, w1b_raw, ALU.add).then_inc(w1_summed, 1)
            dve.wait_ge(w1_hi, 2)
            dve.wait_ge(w1_summed, 1)
            dve.tensor_tensor(w1_l[:], w1a_raw[:, 0:4, :], w1_h[:].bitcast(F32), ALU.subtract).then_inc(w1_ready, 1)
            dve.tensor_tensor(w1_e[0:32, :], w1a_raw[0:32, 4, :], w1_e[0:32, :].bitcast(F32),
                              ALU.subtract).then_inc(w1_ready, 1)
            dve.wait_ge(w1_ready, 2)
            dve.tensor_copy(w1_e[0:16, :], w1a_raw[0:16, 4, :]).then_inc(w1_ready, 1)
            for n in range(2):
                dve.wait_ge(w2_hi, n + 1)
                dve.tensor_tensor(w2_l[:, 16 * n:16 * n + 16, :], w2_raw[:, 16 * n:16 * n + 16, :],
                                  w2_h[:, 16 * n:16 * n + 16, :].bitcast(F32), ALU.subtract).then_inc(w2_lo, 1)

            def pair_mul(i, r, inner, ahead, a):
                if has(i, inner, ahead):
                    dve.wait_ge(rotated, 5 * (i + ahead) + a + 1)
                    wait_count(dve, pair_used, 3 * (i + ahead - 1) + a // 2 + 1)
                    if a == 0:
                        dve.wait_ge(base_ready, i + ahead + 1)
                        wait_count(dve, pair_lo_ready[2], i + ahead)
                    if a == 4:
                        dve.wait_ge(pair_lo_ready[0], i + ahead + 1)
                    dve.tensor_tensor(pair_z[:, a % 4, :], bank[:, ROT + (r + ahead + a) % 2, :], base[:], ALU.mult
                                      ).then_inc(paired, 1)

            def pair_low(i, inner):
                if has(i, inner, 2):
                    dve.wait_ge(pair_hi_ready, 3 * (i + 2) + 1)
                    dve.tensor_tensor(pair_lo[:, 0:2, :], pair_z[:, 0:2, :], pair_hi[:, 0:2, :].bitcast(F32),
                                      ALU.subtract).then_inc(pair_lo_ready[0], 1)

            def last_low(i, inner):
                if has(i, inner, 1):
                    dve.wait_ge(pair_hi_ready, 3 * (i + 1) + 3)
                    dve.tensor_tensor(last_hl[32:64, :], pair_z[32:64, 0, :], last_hl[32:64, :].bitcast(F32),
                                      ALU.subtract).then_inc(pair_lo_ready[2], 1)

            def chain_group(i, r, inner, d, g):
                block_of, slot = (i, r) if d < 2 else (i - 1, r - 1)
                n = DQ * block_of + d
                m = 4 * GROUPS * n + GROUP * g
                if g == 0:
                    dve.wait_ge(scaled_summed, n + 1)
                    if d % 2 == 0:
                        wait_count(dve, chains_halved, 2 * block_of - 1 + d // 2)
                    if isinstance(n, int) and n == 0:
                        dve.wait_ge(w2_lo, 2)
                        dve.wait_ge(w1_ready, 3)
                    dve.wait_ge(x_rows_ready, block_of + 1)
                dve.wait_ge(u_chained_made, GROUPS * n + g + 1)
                for j in range(GROUP):
                    if g:
                        dve.wait_ge(chained, m + j - 3)
                    before = chain[:, d, j, :] if g else scaled_sum[:, d % 2, N * j:N * j + N]
                    dve.scalar_tensor_tensor(chain[:, d, j, :], bank[:, U_CHAINED + g % 2, N * j:N * j + N],
                                             x_rows[:, slot % 8, GROUP * (GROUPS + g) + j, d:d + 1], before,
                                             ALU.mult, ALU.add).then_inc(chained, 1)

            def halve_chains(i, inner, columns):
                if has(i, inner, -1):
                    first = 2 * columns
                    dve.wait_ge(chained, 4 * GROUPS * (DQ * (i - 1) + first + 2))
                    wait_count(dve, out2_made, i - 1)
                    dve.tensor_tensor(halves[:, first:first + 2], chain[:, first:first + 2, 0:2, :],
                                      chain[:, first:first + 2, 2:4, :], ALU.add).then_inc(chains_halved, 1)

            def join_chains(i, inner):
                if has(i, inner, -1):
                    dve.wait_ge(chains_halved, 2 * i)
                    wait_count(dve, out2_summed, i - 1)
                    dve.tensor_tensor(out2[:], halves[:, :, 0, :], halves[:, :, 1, :], ALU.add).then_inc(out2_made, 1)

            def sum_layer2(i, r, inner):
                if not has(i, inner, -1):
                    return
                flat_run = run2[:].rearrange("p d b -> p (d b)")
                source = out2[:].rearrange("p d b -> p (d b)")
                dve.wait_ge(out2_made, i)
                if (r - 1) % PER_TILE == 0:
                    wait_count(dve, folded2, tiles_before(i, r, inner, -1))
                    dve.tensor_scalar(flat_run, source, 0.0, None, ALU.max).then_inc(out2_summed, 1)
                else:
                    dve.wait_ge(out2_summed, i - 1)
                    dve.scalar_tensor_tensor(flat_run, source, 0.0, flat_run, ALU.max, ALU.add
                                             ).then_inc(out2_summed, 1)
                if (r - 1) % PER_TILE == PER_TILE - 1:
                    dve.wait_ge(out2_summed, i)
                    t = tiles_before(i, r, inner, -1)
                    features = feat2_rows[:, t, :] if isinstance(t, int) \
                        else feat2_rows[:, bass.ds(t, 1), :].rearrange("p a n -> p (a n)")
                    fold(t, features, run2, halved2, folded2)

            def fold_layer1(i, r, inner):
                if has(i, inner, 1) and (r + 1) % PER_TILE == PER_TILE - 1:
                    dve.wait_ge(cur_summed, i + 2)
                    t = tiles_before(i, r, inner, 1)
                    cols = bass.ds((i - r) * (P // PER_TILE) + P * ((r + 1) // PER_TILE), P) if inner \
                        else slice(P * t, P * t + P)
                    fold(t, feat1[:, cols], run1, halved1, folded1)
                    dve.wait_ge(folded1, t + 1)
                    dve.memset(run1[:], 0.0).then_inc(cleared1, 1)

            def tiles_before(i, r, inner, ahead):
                return (i - r) // PER_TILE + (r + ahead) // PER_TILE if inner else (i + ahead) // PER_TILE

            def fold(t, features, run, halved, folded):
                dve.tensor_tensor(run[:, 0:2, :], run[:, 0:2, :], run[:, 2:4, :], ALU.add).then_inc(halved, 1)
                dve.wait_ge(halved, t + 1)
                dve.tensor_tensor(features, run[:, 0, :], run[:, 1, :], ALU.add).then_inc(folded, 1)

            def step(i, r, inner):
                for q in range(QUARTERS):
                    if has(i, inner, 0 if q >= 2 * GROUPS else -1):
                        chain_group(i, r, inner, (q // GROUPS + 2) % DQ, q % GROUPS)
                    if q == DVE_AT["multiply_1"]:
                        pair_mul(i, r, inner, 1, 4)
                    if q == DVE_AT["halve"][0]:
                        halve_chains(i, inner, 0)
                    if q == DVE_AT["last_low_1"]:
                        last_low(i, inner)
                    for a in range(4):
                        if q == DVE_AT["multiply_2"][a]:
                            pair_mul(i, r, inner, 2, a)
                    if q == DVE_AT["halve"][1]:
                        halve_chains(i, inner, 1)
                    if q == DVE_AT["rows_low_3"] and has(i, inner, 3):
                        dve.wait_ge(staged_hi, i + 4)
                        k3 = r + 3
                        d0 = DQ * (k3 % PER_TILE)
                        dve.tensor_tensor(split_rows[:, :, F:2 * F],
                                          rows[:, (k3 // PER_TILE) % 2, :, d0:d0 + DQ].rearrange("p f d -> p d f"),
                                          split_rows[:, :, 0:F].bitcast(F32), ALU.subtract).then_inc(staged_lo, 1)
                    if q == DVE_AT["join"]:
                        join_chains(i, inner)
                    if q == DVE_AT["sum"]:
                        sum_layer2(i, r, inner)
                    if q == DVE_AT["pair_low_2"]:
                        pair_low(i, inner)
                    if q == DVE_AT["fold"]:
                        fold_layer1(i, r, inner)

            run_steps(dve, step, 16, 16, 48)

            dve.wait_ge(bias_in, 48)
            for n in range(4):
                dve.wait_ge(top_made, 6 + n + 1)
                dve.tensor_scalar(h1[:, n, COLS:B], bank[:, TOP[1][n], :], b1_sb[:, n:n + 1], 0.0,
                                  ALU.add, ALU.max).then_inc(top_dve, 1)
            for n in range(2):
                dve.wait_ge(top_made, 11 + n + 1)
                dve.tensor_scalar(h2[:, n, COLS:B], bank[:, 2 + n, :], b2_sb[:, n:n + 1], 0.0,
                                  ALU.add, ALU.max).then_inc(top_dve, 1)
            dve.wait_ge(top_made, 14)
            dve.tensor_copy(y_row[:, COLS:B], bank[0:1, 5, :]).then_inc(top_dve, 1)

        @block.tensor
        def _(pe):
            pe.wait_ge(sel_ready, 2)

            def rotate(i, inner, a, parity):
                if has(i, inner, 2):
                    wait_count(pe, paired, 5 * (i + 2) + a - 1)
                    pe.matmul(bank[:, ROT + (parity + a) % 2, :], sel[:, SEL_ROT + a, :], x_pair[:],
                              start=True, stop=True).then_inc(rotated, 1)

            def split_product(acc, wh, wl, hi, lo, start, stop):
                pe.matmul(acc, wh, hi, start=start, stop=False)
                pe.matmul(acc, wl, hi, start=False, stop=False)
                return pe.matmul(acc, wh, lo, start=False, stop=stop)

            def pair_products(i, inner, a):
                if not has(i, inner, 1):
                    return
                k, g, acc = i + 1, a // 2, bank[:, ACC1, :]
                if a == 0:
                    wait_count(pe, cur_hi_ready, k)
                    if isinstance(k, int) and k == 0:
                        pe.wait_ge(w1_ready, 3)
                pe.wait_ge(pair_hi_ready, 3 * k + g + 1)
                pe.wait_ge(pair_lo_ready[g], k + 1)
                if a < 4:
                    mm = split_product(acc, w1_h[:, a, :], w1_l[:, a, :], pair_hi[:, a, :], pair_lo[:, a, :], a == 0, False)
                else:
                    mm = pe.matmul(acc, w1_e[:], last_hl[:], start=False, stop=True)
                if a in (1, 3, 4):
                    mm.then_inc(pair_used, 1)

            def group_products(acc, fields, d, parity):
                return split_product(acc, cur_h[:, parity, d, :], cur_l[:, parity, d, :],
                                     w2_h[:, fields:fields + GROUP, :], w2_l[:, fields:fields + GROUP, :], True, True)

            def scaled_group(i, inner, d, g, parity):
                if has(i, inner, 0):
                    n = GROUPS * (DQ * i + d) + g
                    if d == 0 and g == 0:
                        pe.wait_ge(cur_lo_ready, i + 1)
                        if isinstance(i, int) and i == 0:
                            pe.wait_ge(w2_lo, 2)
                    wait_count(pe, group_scaled, n - 1)
                    group_products(bank[:, U_SCALED + g % 2, :], GROUP * g, d, parity).then_inc(u_scaled_made, 1)

            def chained_group(i, inner, d, g, parity):
                ahead = 0 if d < 2 else -1
                if has(i, inner, ahead):
                    n = GROUPS * (DQ * (i + ahead) + d) + g
                    wait_count(pe, chained, GROUP * (n - 1))
                    group_products(bank[:, U_CHAINED + g % 2, :], GROUP * (GROUPS + g), d,
                                   (parity + ahead) % 2).then_inc(u_chained_made, 1)

            def turn_features(half):
                pe.wait_ge(folded2, 4 * half + 4)
                for t in range(4):
                    mm = pe.matmul(bank[:, ROT + half, P * t:P * t + P], feat2_rows[:, 4 * half + t, :],
                                   ident[:].bitcast(F32), start=True, stop=True)
                mm.then_inc(rows_turned, 1)

            def mlp_first(half, n):
                cols, m = slice(COLS * half, COLS * half + COLS), slice(P * n, P * n + P)
                acc = bank[:, TOP[half][n], :]
                if n == 0:
                    pe.wait_ge(feat2_ready, half + 1)
                pe.matmul(acc, wt1_sb[:, 0, m], feat1[:, cols], start=True, stop=False)
                pe.matmul(acc, wt1_sb[:, 1, m], feat2[:, cols], start=False, stop=False)
                pe.matmul(acc, wt1d_sb[:, m], dense_sb[:, cols], start=False, stop=True).then_inc(top_made, 1)

            def mlp_second(half):
                pe.wait_ge((top_act, top_dve)[half], 4)
                for n in range(2):
                    acc = bank[:, TOP[half][n], :]
                    for c in range(4):
                        mm = pe.matmul(acc, wt2_sb[:, c, P * n:P * n + P], h1[:, c, COLS * half:COLS * half + COLS],
                                       start=(c == 0), stop=(c == 3))
                    mm.then_inc(top_made, 1)

            def mlp_third(half):
                pe.wait_ge((top_act, top_dve)[half], 6)
                for c in range(2):
                    mm = pe.matmul(bank[0:1, 4 + half, :], wt3_sb[:, c:c + 1], h2[:, c, COLS * half:COLS * half + COLS],
                                   start=(c == 0), stop=(c == 1))
                mm.then_inc(top_made, 1)

            def step(i, r, inner):
                parity = r % 2
                if isinstance(i, int) and i == BLOCKS:
                    pe.wait_ge(top_in, 64)
                    pe.wait_ge(folded1, TILES)
                    pe.wait_ge(cur_hi_ready, BLOCKS)
                    pe.wait_ge(group_scaled, GROUPS * DQ * BLOCKS)
                    pe.wait_ge(paired, 5 * BLOCKS)
                    turn_features(0)
                for q in range(QUARTERS):
                    scaled_group(i, inner, q // GROUPS, q % GROUPS, parity)
                    chained_group(i, inner, (q // GROUPS + 2) % DQ, q % GROUPS, parity)
                    if isinstance(i, int) and i == BLOCKS and q in (1, 3, 5, 7):
                        mlp_first(0, q // 2)
                    for a in range(5):
                        if q == PE_AT["pairs_1"][a]:
                            pair_products(i, inner, a)
                        if q == PE_AT["rotate_2"][a]:
                            rotate(i, inner, a, parity)
                    if q == PE_AT["turn_3"] and has(i, inner, 3):
                        pe.wait_ge(staged_lo, i + 4)
                        wait_count(pe, base_ready, i + 3)
                        for d in range(DQ):
                            mm = pe.matmul(bank[:, TURN, P * d:P * d + P], split_rows[:, d, :], ident[:],
                                           start=True, stop=True)
                        mm.then_inc(turned, 1)
                    if q == PE_AT["base_3"] and has(i, inner, 3):
                        pe.wait_ge(x_pair_ready, i + 4)
                        pe.matmul(bank[:, TURN, :], sel[:, SEL_BASE, :], x_pair[:], start=True, stop=True
                                  ).then_inc(base_made, 1)

            run_steps(pe, step, 2, 2, BLOCKS - 4)

            mlp_second(0)
            turn_features(1)
            for n in range(4):
                mlp_first(1, n)
            mlp_third(0)
            mlp_second(1)
            mlp_third(1)


def layouts():
    import numpy as np
    r = np.arange(P)
    kk, m = r // 32, r % 32
    first = np.zeros((P, 5), np.int64)
    second = np.zeros((P, 5), np.int64)
    for a in range(4):
        other = (m + 4 * a + kk) % F
        first[:, a], second[:, a] = m * F + other, other * F + m
    m16 = r % 16
    first[:, 4], second[:, 4] = m16 * F + m16 + 16, (m16 + 16) * F + m16
    sel = np.zeros((P, N_SEL, P), np.float32)
    for half in (0, 32):
        sel[half + m, SEL_BASE, r] = 1.0
        for a in range(4):
            sel[half + (m + 4 * a + kk) % F, SEL_ROT + a, r] = 1.0
        sel[half + (m + 16) % F, SEL_ROT + 4, r] = 1.0
    return first, second, sel, np.eye(P, dtype=np.float32)


def kernel(**inputs):
    import numpy as np
    import concourse.bacc as bacc
    from concourse.bass_utils import run_bass_kernel_spmd

    first, second, sel, eye = layouts()
    f0 = np.asarray(inputs["L0_rec_filter_0"])[0]
    f1 = np.asarray(inputs["L0_rec_filter_1"])[0]
    w1a = f0[first]
    w1b = f0[second]
    w1b[:F, 0] = 0
    w1a[48:, 4] = 0
    w1b[48:, 4] = 0
    w2 = f1.reshape(F, N, N).transpose(1, 0, 2)
    wt1 = np.asarray(inputs["W_top1"])
    arrays = {
        "ids": np.asarray(inputs["ids"]).reshape(TILES, P, F).transpose(1, 0, 2),
        **{f"tbl_{f}": np.asarray(inputs[f"tbl_{f}"]) for f in range(F)},
        "w1a": w1a, "w1b": w1b, "w2": w2, "selectors": sel, "identity": eye,
        "dense": np.asarray(inputs["dense_ctx"]).T,
        "wt1": wt1[:2 * N].reshape(2, P, H1).transpose(1, 0, 2),
        "wt1d": wt1[2 * N:],
        "b1": np.asarray(inputs["b_top1"]).reshape(H1 // P, P).T,
        "wt2": np.asarray(inputs["W_top2"]).reshape(4, P, H2).transpose(1, 0, 2),
        "b2": np.asarray(inputs["b_top2"]).reshape(H2 // P, P).T,
        "wt3": np.asarray(inputs["W_top3"]).reshape(H2 // P, P).T,
    }
    arrays = {name: np.ascontiguousarray(a) for name, a in arrays.items()}
    nc = bacc.Bacc("TRN2", target_bir_lowering=False, num_devices=1)
    ap = {name: nc.dram_tensor(name, a.shape, mybir.dt.from_np(a.dtype), kind="ExternalInput").ap()
          for name, a in arrays.items()}
    y = nc.dram_tensor("y", (1, B), F32, kind="ExternalOutput").ap()
    build_program(nc, ap["ids"], [ap[f"tbl_{f}"] for f in range(F)], ap["w1a"], ap["w1b"], ap["w2"], ap["selectors"],
                  ap["identity"], ap["dense"], ap["wt1"], ap["wt1d"], ap["b1"], ap["wt2"], ap["b2"], ap["wt3"], y)
    r = run_bass_kernel_spmd(nc, [arrays], core_ids=[0])
    return r.results[0]["y"].reshape(B, 1)
```
